# Optimizing a Trainium2 kernel written in Bass

```python
import numpy as np
import jax
import jax.numpy as jnp

def _softmax(x, axis=-1):
    return jax.nn.softmax(x, axis=axis)

def _gelu(x):
    return jax.nn.gelu(x, approximate=True)

def _silu(x):
    return jax.nn.silu(x)

def _sigmoid(x):
    return jax.nn.sigmoid(x)

def _layernorm(x, axis=-1, eps=1e-05):
    m = jnp.mean(x, axis=axis, keepdims=True)
    v = jnp.var(x, axis=axis, keepdims=True)
    return (x - m) / jnp.sqrt(v + eps)

def _scatter_add(tgt, idx, src, axis=0):
    return tgt.at[idx].add(src)

def _segment_sum(src, seg, n):
    return jax.ops.segment_sum(src, seg, n)
kernel_name = 'mk_macaron_d1_jaxref_r8_ac6f80'

def setup_inputs(seed: int=0):
    np.random.seed(seed)
    _w = jnp.asarray

    def _L0_attn_setup():
        import math
        import jax, jax.numpy as jnp
        import numpy as np
        D_MODEL = 128
        NUM_HEADS = 16
        NUM_KV_HEADS = 4
        D_HEAD = D_MODEL // NUM_HEADS
        SEQ = 512
        BATCH = 1
        key = jax.random.key(seed)
        ks = jax.random.split(key, 9)
        s = 0.02
        dkv = NUM_KV_HEADS * D_HEAD
        inp = {'qkv': jax.random.normal(ks[0], (BATCH, SEQ, D_MODEL), jnp.float32), 'Wq': jax.random.normal(ks[1], (D_MODEL, D_MODEL), jnp.float32) * s, 'bq': jnp.zeros((D_MODEL,), jnp.float32), 'Wk': jax.random.normal(ks[2], (D_MODEL, dkv), jnp.float32) * s, 'bk': jnp.zeros((dkv,), jnp.float32), 'Wv': jax.random.normal(ks[3], (D_MODEL, dkv), jnp.float32) * s, 'bv': jnp.zeros((dkv,), jnp.float32), 'Wo': jax.random.normal(ks[4], (D_MODEL, D_MODEL), jnp.float32) * s, 'bo': jnp.zeros((D_MODEL,), jnp.float32), 'slopes': jnp.exp2(-jnp.linspace(0.0, 7.0, NUM_HEADS)).astype(jnp.float32)}
        return inp
    _L0_attn_in = _L0_attn_setup()

    def _L0_ffn_setup():
        import jax, jax.numpy as jnp
        import numpy as np
        H = 128
        I = 64
        E = 8
        K = 2
        SI = I * 2
        B, S = (2, 128)

        def _mlp(x, gw, uw, dw):
            return jax.nn.silu(x @ gw.T) * (x @ uw.T) @ dw.T
        key = jax.random.key(seed)
        ks = jax.random.split(key, 9)
        s = 0.02
        return {'x': jax.random.normal(ks[0], (B, S, H), jnp.float32), 'gate_w': jax.random.normal(ks[1], (E, H), jnp.float32) * s, 'lb_bias': jnp.zeros((E,), jnp.float32), 'expert_gate_w': jax.random.normal(ks[2], (E, I, H), jnp.float32) * s, 'expert_up_w': jax.random.normal(ks[3], (E, I, H), jnp.float32) * s, 'expert_down_w': jax.random.normal(ks[4], (E, H, I), jnp.float32) * s, 'shared_gate_w': jax.random.normal(ks[5], (SI, H), jnp.float32) * s, 'shared_up_w': jax.random.normal(ks[6], (SI, H), jnp.float32) * s, 'shared_down_w': jax.random.normal(ks[7], (H, SI), jnp.float32) * s}
    _L0_ffn_in = _L0_ffn_setup()
    _d = {'L0_attn_qkv': _L0_attn_in['qkv'], 'L0_attn_Wq': _L0_attn_in['Wq'], 'L0_attn_bq': _L0_attn_in['bq'], 'L0_attn_Wk': _L0_attn_in['Wk'], 'L0_attn_bk': _L0_attn_in['bk'], 'L0_attn_Wv': _L0_attn_in['Wv'], 'L0_attn_bv': _L0_attn_in['bv'], 'L0_attn_Wo': _L0_attn_in['Wo'], 'L0_attn_bo': _L0_attn_in['bo'], 'L0_attn_slopes': _L0_attn_in['slopes'], 'L0_ffn_gate_w': _L0_ffn_in['gate_w'], 'L0_ffn_lb_bias': _L0_ffn_in['lb_bias'], 'L0_ffn_expert_gate_w': _L0_ffn_in['expert_gate_w'], 'L0_ffn_expert_up_w': _L0_ffn_in['expert_up_w'], 'L0_ffn_expert_down_w': _L0_ffn_in['expert_down_w'], 'L0_ffn_shared_gate_w': _L0_ffn_in['shared_gate_w'], 'L0_ffn_shared_up_w': _L0_ffn_in['shared_up_w'], 'L0_ffn_shared_down_w': _L0_ffn_in['shared_down_w']}
    _x0 = _d['L0_attn_qkv']
    _d['L0_attn_qkv'] = jax.random.normal(jax.random.fold_in(jax.random.key(seed), 1), (4, 1024, 128), dtype=_x0.dtype)
    del _x0
    return _d

def reference(L0_attn_qkv, L0_attn_Wq, L0_attn_bq, L0_attn_Wk, L0_attn_bk, L0_attn_Wv, L0_attn_bv, L0_attn_Wo, L0_attn_bo, L0_attn_slopes, L0_ffn_gate_w, L0_ffn_lb_bias, L0_ffn_expert_gate_w, L0_ffn_expert_up_w, L0_ffn_expert_down_w, L0_ffn_shared_gate_w, L0_ffn_shared_up_w, L0_ffn_shared_down_w):

    def _L0_attn_ref(qkv, Wq, bq, Wk, bk, Wv, bv, Wo, bo, slopes):
        import math
        import jax, jax.numpy as jnp
        import numpy as np
        D_MODEL = 128
        NUM_HEADS = 16
        NUM_KV_HEADS = 4
        D_HEAD = D_MODEL // NUM_HEADS
        SEQ = 512
        BATCH = 1
        B, S, D = qkv.shape
        H, KVH, dh = (NUM_HEADS, NUM_KV_HEADS, D_HEAD)
        G = H // KVH
        scale = 1.0 / math.sqrt(dh)
        q = (qkv @ Wq + bq).reshape(B, S, H, dh).transpose(0, 2, 1, 3)
        k = (qkv @ Wk + bk).reshape(B, S, KVH, dh).transpose(0, 2, 1, 3)
        v = (qkv @ Wv + bv).reshape(B, S, KVH, dh).transpose(0, 2, 1, 3)
        qg = q.reshape(B, KVH, G, S, dh)
        scores = jnp.einsum('bhgqd,bhkd->bhgqk', qg, k) * scale
        rel = jnp.arange(S, dtype=jnp.float32)[None, :] - jnp.arange(S, dtype=jnp.float32)[:, None]
        bias = slopes.reshape(KVH, G, 1, 1) * rel
        causal = jnp.tril(jnp.ones((S, S), dtype=bool))
        bias = jnp.where(causal, bias, -jnp.inf)
        attn = jax.nn.softmax(scores + bias[None], axis=-1)
        out = jnp.einsum('bhgqk,bhkd->bhgqd', attn, v)
        out = out.reshape(B, H, S, dh).transpose(0, 2, 1, 3).reshape(B, S, D)
        return out @ Wo + bo

    def _L0_ffn_ref(x, gate_w, lb_bias, expert_gate_w, expert_up_w, expert_down_w, shared_gate_w, shared_up_w, shared_down_w):
        import jax, jax.numpy as jnp
        import numpy as np
        H = 128
        I = 64
        E = 8
        K = 2
        SI = I * 2
        B, S = (2, 128)

        def _mlp(x, gw, uw, dw):
            return jax.nn.silu(x @ gw.T) * (x @ uw.T) @ dw.T
        b, s, h = x.shape
        xf = x.reshape(-1, h)
        logits = xf @ gate_w.T + lb_bias
        scores = jax.nn.sigmoid(logits.astype(jnp.float32))
        topw, topi = jax.lax.top_k(scores, K)
        topw = (topw / (topw.sum(-1, keepdims=True) + 1e-08)).astype(x.dtype)
        out = jnp.zeros_like(xf)
        for e in range(E):
            m = topi == e
            sel = m.any(axis=-1)
            cnt = m.sum()
            wmean = (topw * m).sum() / jnp.maximum(cnt, 1).astype(topw.dtype)
            y = _mlp(xf, expert_gate_w[e], expert_up_w[e], expert_down_w[e])
            out = out + jnp.where(sel[:, None], y * wmean, jnp.zeros((), x.dtype))
        out = out.reshape(b, s, h)
        out = out + _mlp(x, shared_gate_w, shared_up_w, shared_down_w)
        return out
    x = L0_attn_qkv
    x = x + 0.5 * _L0_ffn_ref(_layernorm(x, axis=-1), L0_ffn_gate_w, L0_ffn_lb_bias, L0_ffn_expert_gate_w, L0_ffn_expert_up_w, L0_ffn_expert_down_w, L0_ffn_shared_gate_w, L0_ffn_shared_up_w, L0_ffn_shared_down_w)
    x = x + _L0_attn_ref(_layernorm(x, axis=-1), L0_attn_Wq, L0_attn_bq, L0_attn_Wk, L0_attn_bk, L0_attn_Wv, L0_attn_bv, L0_attn_Wo, L0_attn_bo, L0_attn_slopes)
    x = x + 0.5 * _L0_ffn_ref(_layernorm(x, axis=-1), L0_ffn_gate_w, L0_ffn_lb_bias, L0_ffn_expert_gate_w, L0_ffn_expert_up_w, L0_ffn_expert_down_w, L0_ffn_shared_gate_w, L0_ffn_shared_up_w, L0_ffn_shared_down_w)
    return x

_drawn_inputs = setup_inputs


def setup_inputs(seed=0):
    import zlib

    import numpy as np

    out = dict(_drawn_inputs(seed))
    spreads = {'L0_attn_bq': (0.0, 0.8),
     'L0_attn_bk': (0.0, 0.8),
     'L0_attn_bv': (0.0, 0.268),
     'L0_attn_bo': (0.0, 0.1),
     'L0_ffn_lb_bias': (0.0, 0.8)}
    factors = {'L0_attn_Wq': 8.0,
     'L0_attn_Wk': 8.0,
     'L0_attn_Wv': 3.293,
     'L0_attn_slopes': 4.059,
     'L0_ffn_gate_w': 8.0,
     'L0_ffn_expert_gate_w': 8.0,
     'L0_ffn_expert_up_w': 8.0,
     'L0_ffn_expert_down_w': 8.0,
     'L0_ffn_shared_gate_w': 8.0,
     'L0_ffn_shared_up_w': 8.0,
     'L0_ffn_shared_down_w': 8.0}
    for name, (base, spread) in spreads.items():
        noise = np.random.default_rng([zlib.crc32(name.encode()), seed]).standard_normal(out[name].shape)
        drawn = base * np.exp(spread * noise) if base else spread * noise
        out[name] = jnp.asarray(drawn.astype(out[name].dtype))
    for name, factor in factors.items():
        out[name] = (out[name] * factor).astype(out[name].dtype)
    return out
```

```python
from collections import namedtuple
from contextlib import ExitStack

import concourse.bass as bass
from concourse import mybir

F32 = mybir.dt.float32
BF16 = mybir.dt.bfloat16
ALU = mybir.AluOpType
ACT = mybir.ActivationFunctionType
AX = mybir.AxisListType

P = 128
BATCH, SEQ, DM = 4, 1024, 128
TILES = BATCH * SEQ // P
GT = 4
GN = GT * P
GROUPS = TILES // GT
HEADS, KVH, DH = 16, 4, 8
HPG = HEADS // KVH
UNITS = BATCH * KVH
EXPERTS, INTER = 8, 64
HT = (EXPERTS * INTER + 2 * INTER) // P
MT = EXPERTS * INTER // P
EPS = 1e-5
QSCALE = float(DH) ** -0.5

BIAS_ROWS = 15
PROD = 16
QPART = [0, 0, 0, 1, 1, 2]
KPART = [0, 1, 2, 0, 1, 0]
K1 = 96
WROW = 96
K2 = WROW + 2 * HPG
LOADS = 1 + len(QPART) + len(KPART)

HALF = 512
QT = HALF // P
STEPS = [(j, kt) for j in range(2) for kt in range(QT * (j + 1))]
NSTEP = len(STEPS)
NEXP = NSTEP * HPG


def pass1_pieces():
    out = []
    for t in range(SEQ // P):
        w = P * (t % QT + 1)
        per = {1: 4, 2: 2, 3: 1, 4: 1}[t % QT + 1]
        for h in range(0, HPG, per):
            out.append((t, h, per, HALF * (t // QT), w, True))
        if t >= QT:
            out += [(t, h, 1, 0, HALF, False) for h in range(HPG)]
    return out


PIECES = pass1_pieces()
NP1 = len(PIECES)
FIRST_HALF = sum(t < QT for t, *_ in PIECES)
PER_STEP = [0, 1, 2, 3, 4, 4, 4, 4, 4, 4, 4, 4]
assert sum(PER_STEP) == NP1 and len(PER_STEP) == NSTEP and NP1 % 2 == 0 and NEXP % 3 == 0
STEP_START = [sum(PER_STEP[:s]) for s in range(NSTEP)]
W1_STEP = 1
OT1_STEP = 2
OT0_STEP = 7
W0_STEP = 9


FFN_SEMS = ("ve", "rs", "xn", "T", "xT", "gl", "lg", "sig", "sel", "mT", "mk", "G", "U", "sg", "h", "tot", "tops",
            "wds", "Y", "yT", "T2", "x", "ch_up", "ch_down", "ve2", "rs2", "xn2", "Tb", "xTb", "Q", "K", "V", "qf",
            "kf", "pt", "v", "dw0", "dw1", "out")
FfnSems = namedtuple("FfnSems", FFN_SEMS)


def after(eng, sem, value):
    if not isinstance(value, int) or value > 0:
        eng.wait_ge(sem, value)


class Chain:

    def __init__(self, eng, sem):
        self.eng, self.sem = eng, sem
        self.base, self.n = 0, 0

    def at(self, base):
        self.base, self.n = base, 0

    def link(self, ins):
        self.n += 1
        ins.then_inc(self.sem, 1)
        self.eng.wait_ge(self.sem, self.base + self.n)


def over_groups(eng, body):
    body(0, 0, True, False)
    body(1, 1, False, False)
    body(2, 0, False, False)
    with eng.Fori(1, (GROUPS - 2) // 2) as r:
        body(2 * r + 1, 1, False, False)
        body(2 * r + 2, 0, False, False)
    body(GROUPS - 1, 1, False, True)


def over_units(eng, body):
    body(0, 0, True, False)
    with eng.Fori(0, (UNITS - 2) // 2) as r:
        body(2 * r + 1, 1, False, False)
        body(2 * r + 2, 0, False, False)
    body(UNITS - 1, 1, False, True)


def macaron(nc, dram, out):
    ctx = ExitStack()
    with ctx:
        def sb(name, shape, dt=F32):
            return ctx.enter_context(nc.sbuf_tensor(name, shape, dt))

        def sem(name):
            return ctx.enter_context(nc.semaphore(name))

        ps = ctx.enter_context(nc.psum_tensor("ps", [P, 8, 512], F32))

        q_scr = nc.dram_tensor("q_scr", [BATCH, HEADS * DH, 3, SEQ], BF16, kind="Internal").ap()
        k_scr = nc.dram_tensor("k_scr", [BATCH, KVH * DH, 3, SEQ], BF16, kind="Internal").ap()
        bias_scr = nc.dram_tensor("bias_scr", [KVH, BIAS_ROWS, HPG, SEQ], BF16, kind="Internal").ap()
        q_units = q_scr.rearrange("b (g m) r n -> (b g) m r n", g=KVH)
        k_units = k_scr.rearrange("b (g m) r n -> (b g) m r n", g=KVH)

        c128 = sb("c128", [P, 3 * P + HPG + EXPERTS])
        ident = c128[:, 0:P]
        onehot = c128[:, 3 * P:3 * P + HPG]
        rank = c128[:, 3 * P + HPG:3 * P + HPG + EXPERTS]
        cb = sb("cb", [P, 3 * P], BF16)
        ident_b, mask_qk, mask_kq = cb[:, 0:P], cb[:, P:2 * P], cb[:, 2 * P:3 * P]
        krows = sb("krows", [BIAS_ROWS + 1, SEQ])
        qpos = sb("qpos", [HEADS, SEQ])
        esel_f = sb("esel_f", [EXPERTS, MT * P])
        esel = sb("esel", [EXPERTS, MT * P], BF16)
        ones = sb("ones", [P, P])
        mhalf = sb("mhalf", [P, GT])
        wg = sb("wg", [P, HT, P])
        wu = sb("wu", [P, HT, P])
        wd = sb("wd", [P, HT, P])
        wds = sb("wds", [P, HT, P])
        gate_w = sb("gate_w", [P, EXPERTS])
        lb = sb("lb", [P, EXPERTS])
        wq = sb("wq", [P, P])
        wkv = sb("wkv", [P, 2 * KVH * DH])
        wo = sb("wo", [P, P])
        bq = sb("bq", [P, 1])
        bqs = sb("bqs", [P, 1])
        bk = sb("bk", [KVH * DH, 1])
        bv = sb("bv", [P, KVH * DH])
        bo = sb("bo", [P, P])
        slope = sb("slope", [HEADS, 8])

        x = sb("x", [P, TILES, P])
        h_all = sb("h_all", [P, GROUPS, HT, GN])
        stats = sb("stats", [P, GT, 6])
        mv = sb("mv", [P, GT, 2])
        ve = sb("ve", [P, GT])
        rstd = sb("rstd", [P, GT])
        idle = sb("idle", [P, 2])
        xn = sb("xn", [P, GT, P])
        xnT = sb("xnT", [P, 2, GN])
        sg = sb("sg", [P, 2, GN])
        lg = sb("lg", [P, GT, EXPERTS])
        sc = sb("sc", [P, GT, EXPERTS])
        top = sb("top", [P, 8, GT])
        pick = sb("pick", [P, 6, GT, EXPERTS])
        routed = sb("routed", [P, TILES, 2, EXPERTS])
        unsel = sb("unsel", [P, GT, EXPERTS], BF16)
        maskT = sb("maskT", [EXPERTS, 2, GN], BF16)
        tot = sb("tot", [P, 2, EXPERTS])
        wmean = sb("wmean", [P, 3, EXPERTS])
        wrow = sb("wrow", [P, MT])
        yT = sb("yT", [P, 2, GN])

        qf = sb("qf", [P, GN])
        kf = sb("kf", [KVH * DH, GN])
        qres, kres = sg[:, 0, :], sg[0:KVH * DH, 1, :]
        qp = sb("qp", [P, 2, 3, GN], BF16)
        kp = sb("kp", [KVH * DH, 2, 3, GN], BF16)
        v_all = sb("v_all", [P, UNITS, SEQ // P, DH])
        qs = sb("qs", [P, 2, HPG, SEQ], BF16)
        ks = sb("ks", [P, 2, SEQ], BF16)
        vb = sb("vb", [P, 2, SEQ // P, 32])
        mx = sb("mx", [P, 2, 2, QT, HPG])
        mm_ = sb("mm_", [P, QT, HPG])
        wb = sb("wb", [P, QT, 2 * HPG], BF16)
        osb = sb("osb", [P, 2, HALF])
        rden = sb("rden", [P, QT, HPG])
        attn = sb("attn", [P, UNITS, SEQ // P, HPG * DH])
        pr = h_all[:, 0:3, 0:HPG, :]
        bias_st = qs[0:HEADS, :, :, :].rearrange("p a h n -> p (a h) n")

        w_loads = [(c128, "c128"), (krows, "krows"), (qpos, "qpos"), (esel_f, "esel"), (gate_w, "gate_w"),
                   (lb, "lb"), (bq, "bq"), (bk, "bk"), (bv, "bv"), (bo, "bo"), (wg, "wg"), (wu, "wu"), (wd, "wd"),
                   (wq, "wq"), (wkv, "wkv"), (wo, "wo")]

        s_w = sem("s_w")
        s_slope = sem("s_slope")
        s_x0 = sem("s_x0")
        s_init = sem("s_init")
        s_cb = sem("s_cb")
        s_bst = sem("s_bst")
        s_bdma = sem("s_bdma")
        s_dve = sem("s_dve")
        s_kones = sem("s_kones")
        s_ks0 = sem("s_ks0")

        def ffn_sems(n):
            return FfnSems(*[sem(f"f{n}_{name}") for name in FFN_SEMS])

        f1, f2 = ffn_sems(1), ffn_sems(2)
        a_ld = [sem("a_ld0"), sem("a_ld1")]
        a_vb = sem("a_vb")
        a_p1 = sem("a_p1")
        a_rd = sem("a_rd")
        a_w = sem("a_w")
        a_wT = sem("a_wT")
        a_wr = sem("a_wr")
        a_sc = sem("a_sc")
        a_ex = sem("a_ex")
        a_pv = sem("a_pv")
        a_ov = sem("a_ov")
        a_oT = sem("a_oT")
        a_on = sem("a_on")
        a_ch = sem("a_ch")
        o_an, o_T, o_aT, o_y, o_x, o_ch = (sem(f"o_{n}") for n in ("an", "T", "aT", "y", "x", "ch"))

        block = ctx.enter_context(nc.Block())

        def xt(c):
            return x[:, bass.ds(c * GT, GT), :]

        def bank(b):
            return ps[:, b, :]

        @block.sync
        def _(sp):
            xd = dram["x"].rearrange("(c t p) f -> c p t f", t=GT, p=P)
            sp.dma_start(x[:, 0:GT, :], xd[0]).then_inc(s_x0, 16)
            sp.dma_start(slope[:, 0:1], dram["slopes"]).then_inc(s_slope, 16)
            for dst, name in w_loads:
                sp.dma_start(dst[tuple(slice(None) for _ in dst.shape)], dram[name]).then_inc(s_w, 16)
            with sp.Fori(1, GROUPS) as c:
                sp.wait_ge(s_x0, 16 * c)
                sp.dma_start(xt(c), xd[c]).then_inc(s_x0, 16)

            for part in range(3):
                sp.wait_ge(s_bst, part + 1)
                for g in range(KVH):
                    sp.dma_start(bias_scr[g, 5 * part:5 * part + 5].rearrange("r h n -> h r n"),
                                 bias_st[HPG * g:HPG * g + HPG, 0:5, :]).then_inc(s_bdma, 16)
                sp.wait_ge(s_bdma, 16 * KVH * (part + 1))

            def store_parts(c, b, half):
                sp.wait_ge(f1.pt, 2 * c + 2)
                par = half
                n = slice(half * GN, half * GN + GN)
                dw = f1.dw1 if half else f1.dw0
                sp.dma_start(q_scr[b, :, :, n], qp[:, par]).then_inc(dw, 16)
                sp.dma_start(k_scr[b, :, :, n], kp[:, par]).then_inc(dw, 16)

            def load_stack(i, par, g):
                s = a_ld[par]
                sp.dma_start(qs[0:BIAS_ROWS, par, :, :], bias_scr[g]).then_inc(s, 16)
                for n, (a, b) in enumerate(zip(QPART, KPART)):
                    r = PROD + DH * n
                    sp.dma_start(qs[r:r + DH, par, :, :],
                                 q_units[i, :, a, :].rearrange("(h d) n -> d h n", d=DH)).then_inc(s, 16)
                    sp.dma_start(ks[r:r + DH, par, :], k_units[i, :, b, :]).then_inc(s, 16)

            store_parts(0, 0, 0)
            store_parts(1, 0, 1)
            sp.wait_ge(f1.dw0, 32)
            sp.wait_ge(f1.dw1, 32)
            sp.wait_ge(s_init, 1)
            sp.wait_ge(s_ks0, 2)
            sp.wait_ge(s_kones, 1)
            load_stack(0, 0, 0)
            load_stack(1, 1, 1)
            with sp.Fori(1, BATCH) as b:
                store_parts(2 * b, b, 0)
                store_parts(2 * b + 1, b, 1)
            sp.wait_ge(f1.dw0, 32 * BATCH)
            sp.wait_ge(f1.dw1, 32 * BATCH)
            sp.wait_ge(a_pv, NSTEP)
            load_stack(2, 0, 2)
            sp.wait_ge(a_pv, 2 * NSTEP)
            load_stack(3, 1, 3)
            with sp.Fori(1, BATCH) as b:
                for g in range(KVH):
                    sp.wait_ge(a_pv, NSTEP * (KVH * b + g - 1))
                    load_stack(KVH * b + g, g % 2, g)
            od = out.rearrange("(c t p) f -> c p t f", t=GT, p=P)
            with sp.Fori(0, GROUPS) as c:
                sp.wait_ge(f2.x, c + 1)
                sp.dma_start(od[c], xt(c)).then_inc(f2.out, 16)
            sp.wait_ge(f2.out, 16 * GROUPS)

        @block.gpsimd
        def _(pool):
            pool.memset(mhalf[:, :], -0.5)
            pool.memset(ones[:, :], 1.0)
            pool.memset(ks[:, :, :], 0.0)
            pool.memset(vb[:, :, :, :], 0.0).then_inc(s_init, 1)
            pool.wait_ge(s_init, 1)
            pool.memset(ks[WROW:P, :, :], 1.0).then_inc(s_kones, 1)
            pool.wait_ge(s_kones, 1)
            pool.memset(vb[:, :, :, DH:DH + 1], 1.0).then_inc(s_init, 1)

            def rsqrt(ve_sem, xn_sem, rs_sem):
                def body(c, par, first, last):
                    pool.wait_ge(ve_sem, c + 1)
                    after(pool, xn_sem, c)
                    pool.tensor_tensor(rstd[:, :], ve[:, :], mhalf[:, :], ALU.pow).then_inc(rs_sem, 1)
                over_groups(pool, body)

            rsqrt(f1.ve, f1.xn, f1.rs)
            rsqrt(f1.ve2, f1.xn2, f1.rs2)
            rsqrt(f2.ve, f2.xn, f2.rs)

        @block.scalar
        def _(act):
            copy = ACT.Copy
            act.wait_ge(s_w, 16 * len(w_loads))
            act.activation(cb[:, :], c128[:, 0:3 * P], copy).then_inc(s_cb, 1)
            act.activation(esel[:, :], esel_f[:, :], copy).then_inc(s_cb, 1)
            act.activation(bqs[:, :], bq[:, :], copy, scale=QSCALE).then_inc(s_cb, 1)
            act.wait_ge(s_init, 1)
            act.activation(ks[0:BIAS_ROWS + 1, 0, :], krows[:, :], copy)
            act.activation(ks[0:BIAS_ROWS + 1, 1, :], krows[:, :], copy).then_inc(s_ks0, 1)
            act.wait_ge(s_cb, 3)

            def ffn_up(f):
                def xn_T(c, par):
                    act.wait_ge(f.T, c + 1)
                    after(act, f.U, HT * (c - 1))
                    act.activation(xnT[:, par, :], bank(0), copy).then_inc(f.xT, 1)

                def sigmoid(c):
                    act.wait_ge(f.lg, c + 1)
                    after(act, f.sel, c)
                    act.activation(sc[:, :, :], lg[:, :, :], ACT.Sigmoid).then_inc(f.sig, 1)

                def mask_T(c, par):
                    act.wait_ge(f.mT, c + 1)
                    after(act, f.G, HT * (c - 1))
                    act.activation(maskT[:, par, :], ps[0:EXPERTS, 2, 0:GN // 2].bitcast(BF16), copy)\
                       .then_inc(f.mk, 1)

                def silu(c, i, n2):
                    act.wait_ge(f.G, HT * c + i + 1)
                    after(act, f.h, HT * c + i - 1)
                    act.activation(sg[:, n2, :], bank(3 + n2), ACT.Silu).then_inc(f.sg, 1)

                def body(c, par, first, last):
                    for i in range(HT):
                        silu(c, i, (par + i) % 2)
                        if i == 0 and not last:
                            xn_T(c + 1, 1 - par)
                        if i == 2 and not last:
                            sigmoid(c + 1)
                    if not last:
                        mask_T(c + 1, 1 - par)

                xn_T(0, 0)
                sigmoid(0)
                mask_T(0, 0)
                over_groups(act, body)

            def ffn_down(f, qkv):
                def y_T(c, par):
                    act.wait_ge(f.Y, c + 1)
                    after(act, f.T2, c - 1)
                    act.activation(yT[:, par, :], bank(par), copy).then_inc(f.yT, 1)

                def qk(c):
                    act.wait_ge(f.Q, c + 1)
                    after(act, f.pt, 2 * c)
                    act.activation(qf[:, :], bank(5), ACT.Identity, bias=bqs[:, 0:1], scale=QSCALE)\
                       .then_inc(f.qf, 1)
                    act.wait_ge(f.K, c + 1)
                    act.activation(kf[:, :], ps[0:KVH * DH, 6, :], ACT.Identity, bias=bk[:, 0:1]).then_inc(f.kf, 1)

                def body(c, par, first, last):
                    if qkv and not first:
                        qk(c - 1)
                    if not last:
                        y_T(c + 1, 1 - par)
                    if qkv:
                        act.wait_ge(f.Tb, c + 1)
                        after(act, f.V, c - 1)
                        act.activation(xnT[:, par, :], bank(4), copy).then_inc(f.xTb, 1)

                y_T(0, 0)
                over_groups(act, body)
                if qkv:
                    qk(GROUPS - 1)

            def write_rows(i, par, j):
                act.wait_ge(a_wT, 2 * i + j + 1)
                for h in range(HPG):
                    ins = act.activation(qs[WROW:K2, par, h, HALF * j:HALF * j + HALF],
                                         ps[WROW:K2, 7, 0:HALF // 2].bitcast(BF16), copy,
                                         scale=onehot[WROW:K2, h:h + 1])
                ins.then_inc(a_wr, 1)

            def out_evac(i, j):
                act.wait_ge(a_pv, NSTEP * i + (QT if j == 0 else NSTEP))
                after(act, a_oT, 2 * i + j - 1)
                act.activation(osb[:, j, :], bank(5 + j), copy).then_inc(a_ov, 1)

            def attention():
                write_rows(0, 0, 0)

                def body(i, par, first, last):
                    for s, (j, kt) in enumerate(STEPS):
                        lo = max(0, kt - QT * j) * P
                        after(act, a_pv, NSTEP * i + s - 2)
                        for h in range(HPG):
                            m = HPG * s + h
                            act.wait_ge(a_sc, NEXP * i + m + 1)
                            act.activation(pr[:, s % 3, h, lo:HALF], ps[:, 2 + m % 3, lo:HALF], ACT.Exp)\
                               .then_inc(a_ex, 1)
                        if s == 0 and not first:
                            out_evac(i - 1, 1)
                        if s == W1_STEP + 1:
                            write_rows(i, par, 1)
                        if s == QT + 1:
                            out_evac(i, 0)
                        if s == W0_STEP + 1 and not last:
                            write_rows(i + 1, 1 - par, 0)

                over_units(act, body)
                out_evac(UNITS - 1, 1)

            def out_proj():
                def body(c, par, first, last):
                    act.wait_ge(o_T, c + 1)
                    after(act, o_y, c - 1)
                    act.activation(yT[:, par, :], bank(par), copy).then_inc(o_aT, 1)
                over_groups(act, body)

            ffn_up(f1)
            ffn_down(f1, True)
            attention()
            out_proj()
            ffn_up(f2)
            ffn_down(f2, False)

        @block.vector
        def _(dve):
            V = ALU

            def bias_rows():
                ch = Chain(dve, s_dve)
                dve.wait_ge(s_slope, 16)
                dve.wait_ge(s_w, 16 * len(w_loads))
                dve.wait_ge(s_init, 1)
                sb16 = wb[0:HEADS, 0, 0:3]
                for part in range(3):
                    ch.link(dve.tensor_copy(sb16[:, part:part + 1], slope[:, part:part + 1]))
                    if part < 2:
                        ch.link(dve.tensor_tensor(slope[:, part + 1:part + 2], slope[:, part:part + 1],
                                                  sb16[:, part:part + 1], V.subtract))
                    ch.link(dve.tensor_scalar(slope[:, 4 + part:5 + part], sb16[:, part:part + 1], -1.0, None,
                                              V.mult))
                t, rest = yT[0:HEADS, :, :], xnT[0:HEADS, :, :]
                tf = t.rearrange("p a n -> p (a n)")
                rf = rest.rearrange("p a n -> p (a n)")
                for part in range(3):
                    if part:
                        dve.wait_ge(s_bdma, 16 * KVH * part)
                    ch.link(dve.tensor_scalar(tf, qpos[:, :], slope[:, 4 + part:5 + part], None, V.mult))
                    ch.link(dve.tensor_copy(bias_st[:, 2, :], tf))
                    ch.link(dve.tensor_tensor(rf, tf, bias_st[:, 2, :], V.subtract))
                    ch.link(dve.tensor_copy(bias_st[:, 3, :], rf))
                    ch.link(dve.tensor_tensor(bias_st[:, 4, :], rf, bias_st[:, 3, :], V.subtract))
                    ch.link(dve.tensor_scalar(bias_st[:, 0, :], qpos[:, :], 0.0, slope[:, 4 + part:5 + part],
                                              V.mult, V.subtract))
                    dve.tensor_copy(bias_st[:, 1, :], bias_st[:, 0, :]).then_inc(s_bst, 1)
                dve.wait_ge(s_bdma, 16 * KVH * 3)
                dve.memset(qs[0:64, :, :, :], 0.0)
                dve.memset(qs[64:96, :, :, :], 0.0).then_inc(s_ks0, 1)

            def layer_norm(c, ch, s_ve, s_rs, s_T, s_xn):
                dve.memset(idle[:, 0:1], 0.0)
                for t in range(GT):
                    ins = dve.bn_stats(stats[:, t, :], x[:, c * GT + t, :])
                ch.link(ins)
                dve.memset(idle[:, 1:2], 0.0)
                for t in range(GT):
                    ins = dve.bn_aggr(mv[:, t, :], stats[:, t, :])
                ch.link(ins)
                dve.tensor_scalar(ve[:, :], mv[:, :, 1], EPS, None, V.add).then_inc(s_ve, 1)
                after(dve, s_T, c)
                dve.wait_ge(s_rs, c + 1)
                for t in range(GT):
                    ins = dve.tensor_scalar(xn[:, t, :], x[:, c * GT + t, :], mv[:, t, 0:1], rstd[:, t:t + 1],
                                            V.subtract, V.mult)
                ins.then_inc(s_xn, 1)

            def ffn_up(f, load_sem):
                ch = Chain(dve, f.ch_up)
                LN_LINKS, TOP_LINKS = 2, 17

                def norm(c):
                    ch.at((LN_LINKS + TOP_LINKS) * c)
                    if load_sem is not None:
                        dve.wait_ge(load_sem, 16 * c + 16)
                    layer_norm(c, ch, f.ve, f.rs, f.T, f.xn)

                def logits(c):
                    dve.wait_ge(f.gl, c + 1)
                    dve.tensor_tensor(lg[:, :, :], ps[:, 1, 0:GT * EXPERTS].rearrange("p (t e) -> p t e", t=GT),
                                      lb[:, None, :].broadcast_to([P, GT, EXPERTS]), V.add).then_inc(f.lg, 1)

                def topk(c):
                    ch.at((LN_LINKS + TOP_LINKS) * c + LN_LINKS)
                    dve.wait_ge(f.sig, c + 1)
                    rk = rank[:, None, :].broadcast_to([P, GT, EXPERTS])

                    def wide(a):
                        return a[:, :, None].broadcast_to([P, GT, EXPERTS])
                    pick1, pick2, s2, eq, wt = (pick[:, n] for n in range(5))
                    m1, m2, r1, r2, den, w1, w2 = (top[:, n] for n in range(7))

                    def first_max(scores, m, r, sel):
                        ch.link(dve.tensor_reduce(m, scores, AX.X, V.max))
                        ch.link(dve.tensor_tensor(eq, scores, wide(m), V.is_equal))
                        ch.link(dve.tensor_tensor(eq, eq, rk, V.mult))
                        ch.link(dve.tensor_reduce(r, eq, AX.X, V.max))
                        ch.link(dve.tensor_tensor(sel, rk, wide(r), V.is_equal))
                    first_max(sc[:, :, :], m1, r1, pick1)
                    ch.link(dve.scalar_tensor_tensor(out=s2, in0=pick1, scalar=-4.0, in1=sc[:, :, :],
                                                     op0=V.mult, op1=V.add))
                    first_max(s2, m2, r2, pick2)
                    both = routed[:, bass.ds(c * GT, GT), 1, :]
                    after(dve, f.mT, c)
                    dve.tensor_tensor(both, pick1, pick2, V.add)
                    dve.scalar_tensor_tensor(out=unsel[:, :, :], in0=pick1, scalar=-1.0, in1=pick2,
                                             op0=V.add, op1=V.add).then_inc(f.sel, 1)
                    ch.link(dve.tensor_tensor(den, m1, m2, V.add))
                    ch.link(dve.tensor_scalar(den, den, 1e-8, None, V.add))
                    ch.link(dve.reciprocal(den, den))
                    dve.tensor_tensor(w1, m1, den, V.mult)
                    ch.link(dve.tensor_tensor(w2, m2, den, V.mult))
                    dve.tensor_tensor(wt, pick1, wide(w1), V.mult)
                    ch.link(dve.tensor_tensor(s2, pick2, wide(w2), V.mult))
                    ch.link(dve.tensor_tensor(routed[:, bass.ds(c * GT, GT), 0, :], wt, s2, V.add))
                    assert ch.n == TOP_LINKS

                def hidden(c, i, n2):
                    dve.wait_ge(f.U, HT * c + i + 1)
                    dve.wait_ge(f.sg, HT * c + i + 1)
                    dve.tensor_tensor(h_all[:, c, i, :], bank(5 + n2), sg[:, n2, :], V.mult).then_inc(f.h, 1)

                def body(c, par, first, last):
                    if not last:
                        norm(c + 1)
                    for i in range(HT):
                        hidden(c, i, (par + i) % 2)
                        if i == 2 and not last:
                            logits(c + 1)
                            topk(c + 1)

                norm(0)
                logits(0)
                topk(0)
                over_groups(dve, body)
                ch.at((LN_LINKS + TOP_LINKS) * GROUPS)
                dve.tensor_reduce(tot[:, :, :], routed[:, :, :, :].rearrange("p t w e -> p w e t"), AX.X, V.add)\
                   .then_inc(f.tot, 1)
                dve.wait_ge(f.tops, 1)
                t2 = ps[:, 1, 0:2 * EXPERTS].rearrange("p (w e) -> p w e", w=2)
                ch.link(dve.tensor_scalar(wmean[:, 1, :], t2[:, 1, :], 1.0, None, V.max))
                ch.link(dve.reciprocal(wmean[:, 2, :], wmean[:, 1, :]))
                ch.link(dve.scalar_tensor_tensor(out=wmean[:, 0, :], in0=t2[:, 0, :], scalar=0.5,
                                                 in1=wmean[:, 2, :], op0=V.mult, op1=V.mult))
                for k in range(2):
                    rows = slice(k * INTER, k * INTER + INTER)
                    ins = dve.tensor_copy(wrow[rows, :], wmean[rows, 0, k:EXPERTS:2])
                ch.link(ins)
                for i in range(MT):
                    dve.tensor_scalar(wds[:, i, :], wd[:, i, :], wrow[:, i:i + 1], None, V.mult)
                dve.tensor_scalar(wds[:, MT, :], wd[:, MT, :], 0.5, None, V.mult).then_inc(f.wds, 1)

            def ffn_down(f, qkv):
                ch = Chain(dve, f.ch_down)
                LN_LINKS, SPLIT_LINKS = 2, 6
                LINKS = LN_LINKS + SPLIT_LINKS

                def split(src, rest, parts, done, ready, c):
                    dve.wait_ge(ready, c + 1)
                    ch.link(dve.tensor_copy(parts[:, 0, :], src))
                    ch.link(dve.tensor_tensor(rest, src, parts[:, 0, :], V.subtract))
                    ch.link(dve.tensor_copy(parts[:, 1, :], rest))
                    dve.tensor_tensor(parts[:, 2, :], rest, parts[:, 1, :], V.subtract).then_inc(done, 1)

                def projections(c, par, tail=False):
                    after(dve, f.dw1 if par else f.dw0, 16 * (c - par))
                    split(qf[:, :], qres, qp[:, par], f.pt, f.qf, c)
                    split(kf[:, :], kres, kp[:, par], f.pt, f.kf, c)
                    dve.wait_ge(f.V, c + 1)

                def values(c, b, half):
                    vin = ps[:, 7, 0:GT * KVH * DH].rearrange("p (t g d) -> p g t d", t=GT, g=KVH)
                    vout = v_all[:, bass.ds(KVH * b, KVH), GT * half:GT * half + GT, :]
                    for t in range(GT):
                        ins = dve.tensor_tensor(vout[:, :, t, :], vin[:, :, t, :],
                                                bv[:, :].rearrange("p (g d) -> p g d", g=KVH), V.add)
                    ins.then_inc(f.v, 1)

                def body(c, par, first, last, b=None):
                    dve.wait_ge(f.T2, c + 1)
                    ins = dve.tensor_tensor(xt(c), xt(c),
                                            bank(2 + par).rearrange("p (t f) -> p t f", t=GT), V.add)
                    ins.then_inc(f.x, 1)
                    if qkv:
                        ch.at(0 if first else LINKS * c - SPLIT_LINKS)
                        dve.wait_ge(f.x, c + 1)
                        layer_norm(c, ch, f.ve2, f.rs2, f.Tb, f.xn2)
                        if not first:
                            prev(c, par)

                def prev(c, par):
                    projections(c - 1, 1 - par)

                if not qkv:
                    over_groups(dve, body)
                    return
                body(0, 0, True, False)
                body(1, 1, False, False)
                values(0, 0, 0)
                body(2, 0, False, False)
                values(1, 0, 1)
                with dve.Fori(1, (GROUPS - 2) // 2) as r:
                    body(2 * r + 1, 1, False, False)
                    values(2 * r, r, 0)
                    body(2 * r + 2, 0, False, False)
                    values(2 * r + 1, r, 1)
                body(GROUPS - 1, 1, False, True)
                values(GROUPS - 2, BATCH - 1, 0)
                ch.at(LINKS * GROUPS - SPLIT_LINKS)
                projections(GROUPS - 1, 1)
                values(GROUPS - 1, BATCH - 1, 1)

            def attention():
                ch = Chain(dve, a_ch)

                def load_v(i, par):
                    after(dve, a_pv, NSTEP * (i - 1))
                    dve.tensor_copy(vb[:, par, :, 0:DH], v_all[:, i, :, :]).then_inc(a_vb, 1)

                def reduce(i, n):
                    t, h, per, k0, w, diag = PIECES[n]
                    dve.wait_ge(a_p1, NP1 * i + n + 1)
                    src = ps[:, n % 2, 0:per * w].rearrange("p (h w) -> p h w", h=per)
                    dve.tensor_reduce(mx[:, t // QT, 0 if diag else 1, t % QT, h:h + per], src, AX.X, V.max)\
                       .then_inc(a_rd, 1)

                def maxima(i, j):
                    n = FIRST_HALF if j == 0 else NP1
                    dve.wait_ge(a_rd, NP1 * i + n)
                    m = mx[:, 0, 0]
                    if j:
                        m = mm_[:, :, :]
                        ch.link(dve.tensor_tensor(m, mx[:, 1, 0], mx[:, 1, 1], V.max))
                    after(dve, a_wT, 2 * i + j)
                    ch.link(dve.tensor_scalar(wb[:, :, 0:HPG], m, -1.0, None, V.mult))
                    dve.scalar_tensor_tensor(out=wb[:, :, HPG:2 * HPG], in0=m, scalar=-1.0, in1=wb[:, :, 0:HPG],
                                             op0=V.mult, op1=V.subtract).then_inc(a_w, 1)

                def normalise(i, j):
                    after(dve, a_on, 2 * i + j)
                    dve.wait_ge(a_oT, 2 * i + j + 1)
                    o = bank(5 + j).rearrange("p (t h e) -> p t h e", t=QT, h=HPG)
                    ch.link(dve.reciprocal(rden[:, :, :], o[:, :, :, DH]))
                    for t in range(QT):
                        ins = dve.tensor_tensor(
                            attn[:, i, QT * j + t, :].rearrange("p (h d) -> p h d", h=HPG), o[:, t, :, 0:DH],
                            rden[:, t, :, None].broadcast_to([P, HPG, DH]), V.mult)
                    ins.then_inc(a_on, 1)

                CH_UNIT = 1 + 1 + 1 + 2
                load_v(0, 0)
                for n in range(NP1):
                    reduce(0, n)
                    if n == FIRST_HALF - 1:
                        maxima(0, 0)
                maxima(0, 1)
                START = 3

                def body(i, par, first, last):
                    ch.at(START + CH_UNIT * i - (0 if first else 1))
                    if not last:
                        load_v(i + 1, 1 - par)
                    for s in range(NSTEP):
                        if not last:
                            for n in range(STEP_START[s], STEP_START[s] + PER_STEP[s]):
                                reduce(i + 1, n)
                                if n == FIRST_HALF - 1:
                                    maxima(i + 1, 0)
                        if s == OT1_STEP and not first:
                            normalise(i - 1, 1)
                        if s == OT0_STEP:
                            normalise(i, 0)
                    if not last:
                        maxima(i + 1, 1)

                over_units(dve, body)
                normalise(UNITS - 1, 1)

            def out_proj():
                ch = Chain(dve, o_ch)

                def gather(c, b, half, par):
                    after(dve, o_T, c - 1)
                    src = attn[:, bass.ds(KVH * b, KVH), GT * half:GT * half + GT, :]
                    dst = sg[:, par, :].rearrange("p (t g e) -> p g t e", t=GT, g=KVH)
                    for t in range(GT):
                        ins = dve.tensor_copy(dst[:, :, t, :], src[:, :, t, :])
                    ins.then_inc(o_an, 1)

                def residual(c, par):
                    ch.at(c)
                    dve.wait_ge(o_y, c + 1)
                    ch.link(dve.tensor_tensor(xt(c), xt(c), bank(2 + par).rearrange("p (t f) -> p t f", t=GT), V.add))
                    dve.tensor_tensor(xt(c), xt(c), bo[:, None, :].broadcast_to([P, GT, P]), V.add).then_inc(o_x, 1)

                dve.wait_ge(a_on, 2 * UNITS)
                gather(0, 0, 0, 0)
                gather(1, 0, 1, 1)
                with dve.Fori(0, BATCH - 1) as b:
                    residual(2 * b, 0)
                    gather(2 * b + 2, b + 1, 0, 0)
                    residual(2 * b + 1, 1)
                    gather(2 * b + 3, b + 1, 1, 1)
                residual(GROUPS - 2, 0)
                residual(GROUPS - 1, 1)
                dve.wait_ge(o_x, GROUPS)

            bias_rows()
            ffn_up(f1, s_x0)
            ffn_down(f1, True)
            attention()
            out_proj()
            ffn_up(f2, None)
            ffn_down(f2, False)

        @block.tensor
        def _(pe):
            def mm(o, l, r, start=True, stop=True):
                return pe.matmul(o, l, r, start=start, stop=stop, skip_group_check=True)

            def turn(src, b):
                for t in range(GT):
                    ins = pe.transpose(ps[:, b, t * P:(t + 1) * P], src(t), ident)
                return ins

            def ffn_up(f):
                def xn_T(c):
                    pe.wait_ge(f.xn, c + 1)
                    after(pe, f.xT, c)
                    turn(lambda t: xn[:, t, :], 0).then_inc(f.T, 1)

                def gate(c, par):
                    pe.wait_ge(f.xT, c + 1)
                    after(pe, f.lg, c)
                    for t in range(GT):
                        ins = mm(ps[:, 1, EXPERTS * t:EXPERTS * t + EXPERTS], xnT[:, par, t * P:(t + 1) * P],
                                 gate_w[:, :])
                    ins.then_inc(f.gl, 1)

                def mask_T(c):
                    pe.wait_ge(f.sel, c + 1)
                    after(pe, f.mk, c)
                    o = ps[0:EXPERTS, 2, 0:GN // 2].bitcast(BF16)
                    for t in range(GT):
                        ins = pe.transpose(o[:, t * P:(t + 1) * P], unsel[:, t, :], ident_b)
                    ins.then_inc(f.mT, 1)

                def up(c, i, n2, par):
                    after(pe, f.sg, HT * c + i - 1)
                    routed_tile = i < MT
                    ins = mm(bank(3 + n2), wg[:, i, :], xnT[:, par, :], stop=not routed_tile)
                    if routed_tile:
                        ins = mm(bank(3 + n2), esel[:, i * P:(i + 1) * P], maskT[:, par, :], start=False)
                    ins.then_inc(f.G, 1)
                    after(pe, f.h, HT * c + i - 1)
                    mm(bank(5 + n2), wu[:, i, :], xnT[:, par, :]).then_inc(f.U, 1)

                def body(c, par, first, last):
                    pe.wait_ge(f.mk, c + 1)
                    for i in range(HT):
                        up(c, i, (par + i) % 2, par)
                        if i == 0 and not last:
                            xn_T(c + 1)
                        if i == 2 and not last:
                            gate(c + 1, 1 - par)
                    if not last:
                        mask_T(c + 1)

                xn_T(0)
                gate(0, 0)
                mask_T(0)
                over_groups(pe, body)
                pe.wait_ge(f.tot, 1)
                mm(ps[:, 1, 0:2 * EXPERTS], ones[:, :], tot[:, :, :].rearrange("p w e -> p (w e)"))\
                    .then_inc(f.tops, 1)

            def ffn_down(f, qkv):
                def down(c, par):
                    after(pe, f.yT, c - 1)
                    for i in range(HT):
                        ins = mm(bank(par), wds[:, i, :], h_all[:, c, i, :], start=(i == 0), stop=(i == HT - 1))
                    ins.then_inc(f.Y, 1)

                def project(c, par):
                    pe.wait_ge(f.xTb, c + 1)
                    after(pe, f.qf, c)
                    mm(bank(5), wq[:, :], xnT[:, par, :]).then_inc(f.Q, 1)
                    after(pe, f.kf, c)
                    mm(ps[0:KVH * DH, 6, :], wkv[:, 0:KVH * DH], xnT[:, par, :]).then_inc(f.K, 1)
                    after(pe, f.v, c)
                    w = KVH * DH
                    for t in range(GT):
                        ins = mm(ps[:, 7, w * t:w * t + w], xnT[:, par, t * P:(t + 1) * P], wkv[:, w:2 * w])
                    ins.then_inc(f.V, 1)

                def body(c, par, first, last):
                    pe.wait_ge(f.yT, c + 1)
                    after(pe, f.x, c - 1)
                    turn(lambda t: yT[:, par, t * P:(t + 1) * P], 2 + par).then_inc(f.T2, 1)
                    if qkv and not first:
                        project(c - 1, 1 - par)
                    if not last:
                        down(c + 1, 1 - par)
                    if qkv:
                        pe.wait_ge(f.xn2, c + 1)
                        after(pe, f.xTb, c)
                        turn(lambda t: xn[:, t, :], 4).then_inc(f.Tb, 1)

                pe.wait_ge(f.wds, 1)
                down(0, 0)
                over_groups(pe, body)
                if qkv:
                    project(GROUPS - 1, 1)

            def piece(i, n, par):
                t, h0, per, k0, w, diag = PIECES[n]
                if n >= 2:
                    pe.wait_ge(a_rd, NP1 * i + n - 1)
                else:
                    after(pe, a_rd, NP1 * i + n - 1)
                for k in range(per):
                    o = ps[:, n % 2, k * w:k * w + w]
                    ins = mm(o, qs[0:K1, par, h0 + k, t * P:(t + 1) * P], ks[0:K1, par, k0:k0 + w], stop=not diag)
                    if diag:
                        ins = mm(ps[:, n % 2, k * w + w - P:k * w + w], ident_b, mask_qk, start=False)
                ins.then_inc(a_p1, 1)

            def maxima_T(i, j):
                pe.wait_ge(a_w, 2 * i + j + 1)
                after(pe, a_wr, 2 * i + j)
                o = ps[WROW:K2, 7, 0:HALF // 2].bitcast(BF16)
                for t in range(QT):
                    ins = pe.transpose(o[:, t * P:(t + 1) * P], wb[:, t, :], ident_b)
                ins.then_inc(a_wT, 1)

            def out_T(i, j):
                pe.wait_ge(a_ov, 2 * i + j + 1)
                turn(lambda t: osb[:, j, t * P:(t + 1) * P], 5 + j).then_inc(a_oT, 1)

            def score(i, s, h, par):
                j, kt = STEPS[s]
                m = HPG * s + h
                lo = max(0, kt - QT * j) * P
                diag = kt >= QT * j
                if m >= 3:
                    pe.wait_ge(a_ex, NEXP * i + m - 2)
                else:
                    after(pe, a_ex, NEXP * i + m - 2)
                o = ps[:, 2 + m % 3, lo:HALF]
                ins = mm(o, ks[0:K2, par, kt * P:(kt + 1) * P], qs[0:K2, par, h, HALF * j + lo:HALF * j + HALF],
                         stop=not diag)
                if diag:
                    ins = mm(ps[:, 2 + m % 3, lo:lo + P], ident_b, mask_kq, start=False)
                ins.then_inc(a_sc, 1)

            def times_v(i, s, par):
                j, kt = STEPS[s]
                lo = max(0, kt - QT * j) * P
                last = kt == QT * (j + 1) - 1
                pe.wait_ge(a_ex, NEXP * i + HPG * (s + 1))
                if kt == 0:
                    after(pe, a_on, 2 * i + j - 1)
                for h in range(HPG):
                    ins = mm(ps[32 * h:32 * h + 32, 5 + j, lo:HALF], vb[:, par, kt, :], pr[:, s % 3, h, lo:HALF],
                             start=(kt == 0), stop=last)
                ins.then_inc(a_pv, 1)

            def attention():
                pe.wait_ge(a_ld[0], 16 * LOADS)
                for n in range(NP1):
                    piece(0, n, 0)
                maxima_T(0, 0)

                def body(i, par, first, last):
                    pe.wait_ge(a_wr, 2 * i + 1)
                    pe.wait_ge(a_vb, i + 1)
                    for h in range(HPG):
                        score(i, 0, h, par)
                    for s in range(NSTEP):
                        todo = [] if last else list(range(STEP_START[s], STEP_START[s] + PER_STEP[s]))
                        if s + 1 == QT:
                            pe.wait_ge(a_wr, 2 * i + 2)
                        if todo and todo[0] == 0:
                            next_stack(i, par)
                        for h in range(HPG):
                            if s + 1 < NSTEP:
                                score(i, s + 1, h, par)
                            if h < len(todo):
                                piece(i + 1, todo[h], 1 - par)
                        times_v(i, s, par)
                        if s == W1_STEP:
                            maxima_T(i, 1)
                        if s == OT1_STEP and not first:
                            out_T(i - 1, 1)
                        if s == OT0_STEP:
                            out_T(i, 0)
                        if s == W0_STEP and not last:
                            maxima_T(i + 1, 0)

                def next_stack(i, par):
                    pe.wait_ge(a_ld[1 - par], 8 * LOADS * (i + 3 if par else i + 2))

                over_units(pe, body)
                out_T(UNITS - 1, 1)

            def out_proj():
                def body(c, par, first, last):
                    pe.wait_ge(o_an, c + 1)
                    after(pe, o_aT, c - 1)
                    turn(lambda t: sg[:, par, t * P:(t + 1) * P], par).then_inc(o_T, 1)
                    pe.wait_ge(o_aT, c + 1)
                    after(pe, o_x, c - 1)
                    for t in range(GT):
                        ins = mm(ps[:, 2 + par, t * P:(t + 1) * P], yT[:, par, t * P:(t + 1) * P], wo[:, :])
                    ins.then_inc(o_y, 1)
                over_groups(pe, body)

            pe.wait_ge(s_w, 16 * len(w_loads))
            pe.wait_ge(s_cb, 3)
            pe.wait_ge(s_init, 2)
            ffn_up(f1)
            ffn_down(f1, True)
            attention()
            out_proj()
            ffn_up(f2)
            ffn_down(f2, False)


def kernel(L0_attn_qkv, L0_attn_Wq, L0_attn_bq, L0_attn_Wk, L0_attn_bk, L0_attn_Wv, L0_attn_bv, L0_attn_Wo,
           L0_attn_bo, L0_attn_slopes, L0_ffn_gate_w, L0_ffn_lb_bias, L0_ffn_expert_gate_w, L0_ffn_expert_up_w,
           L0_ffn_expert_down_w, L0_ffn_shared_gate_w, L0_ffn_shared_up_w, L0_ffn_shared_down_w):
    import numpy as np
    import concourse.bacc as bacc
    from concourse.bass_utils import run_bass_kernel_spmd

    def arr(a):
        return np.ascontiguousarray(np.asarray(a))

    at = np.arange(P)
    c128 = np.zeros((P, 3 * P + HPG + EXPERTS), np.float32)
    c128[:, 0:P] = np.eye(P)
    c128[:, P:2 * P] = np.where(at[None, :] > at[:, None], -1e30, 0.0)
    c128[:, 2 * P:3 * P] = np.where(at[:, None] > at[None, :], -1e30, 0.0)
    for h in range(HPG):
        c128[[WROW + h, WROW + HPG + h], 3 * P + h] = 1.0
    c128[:, 3 * P + HPG:] = np.arange(EXPERTS, 0, -1)
    pos = np.arange(SEQ, dtype=np.float32)
    krows = np.zeros((BIAS_ROWS + 1, SEQ), np.float32)
    for part in range(3):
        krows[5 * part] = pos - pos % 8
        krows[5 * part + 1] = pos % 8
        krows[5 * part + 2:5 * part + 5] = 1.0
    esel = np.zeros((EXPERTS, MT, P), np.float32)
    for e in range(EXPERTS):
        esel[e, e // 2, (e % 2) * INTER:(e % 2) * INTER + INTER] = 2.0 ** 30

    def up(experts, shared):
        w = np.concatenate([arr(experts).reshape(EXPERTS * INTER, DM), arr(shared)], 0)
        return arr(w.T.reshape(DM, HT, P))

    down = np.concatenate([arr(L0_ffn_expert_down_w).transpose(0, 2, 1).reshape(EXPERTS * INTER, DM),
                           arr(L0_ffn_shared_down_w).T], 0)
    data = {
        "x": arr(L0_attn_qkv).reshape(BATCH * SEQ, DM),
        "slopes": arr(L0_attn_slopes).reshape(HEADS, 1),
        "c128": c128, "krows": krows, "qpos": arr(np.broadcast_to(pos, (HEADS, SEQ))),
        "esel": esel.reshape(EXPERTS, MT * P),
        "gate_w": arr(arr(L0_ffn_gate_w).T),
        "lb": arr(np.broadcast_to(arr(L0_ffn_lb_bias), (P, EXPERTS))),
        "bq": arr(L0_attn_bq).reshape(DM, 1), "bk": arr(L0_attn_bk).reshape(KVH * DH, 1),
        "bv": arr(np.broadcast_to(arr(L0_attn_bv), (P, KVH * DH))),
        "bo": arr(np.broadcast_to(arr(L0_attn_bo), (P, DM))),
        "wg": up(L0_ffn_expert_gate_w, L0_ffn_shared_gate_w),
        "wu": up(L0_ffn_expert_up_w, L0_ffn_shared_up_w),
        "wd": arr(down.reshape(HT, P, DM).transpose(1, 0, 2)),
        "wq": arr(L0_attn_Wq), "wkv": arr(np.concatenate([arr(L0_attn_Wk), arr(L0_attn_Wv)], 1)),
        "wo": arr(L0_attn_Wo),
    }
    nc = bacc.Bacc("TRN2", target_bir_lowering=False, num_devices=1)
    dram = {n: nc.dram_tensor(f"in_{n}", a.shape, F32, kind="ExternalInput").ap() for n, a in data.items()}
    out = nc.dram_tensor("out", (BATCH * SEQ, DM), F32, kind="ExternalOutput").ap()
    macaron(nc, dram, out)
    r = run_bass_kernel_spmd(nc, [{f"in_{n}": a for n, a in data.items()}], core_ids=[0])
    return r.results[0]["out"].reshape(BATCH, SEQ, DM)
```

```python
from collections import namedtuple
from contextlib import ExitStack

import concourse.bass as bass
from concourse import mybir

F32 = mybir.dt.float32
BF16 = mybir.dt.bfloat16
ALU = mybir.AluOpType
ACT = mybir.ActivationFunctionType
AX = mybir.AxisListType

P = 128
BATCH, SEQ, DM = 4, 1024, 128
TILES = BATCH * SEQ // P
GT = 4
GN = GT * P
GROUPS = TILES // GT
HEADS, KVH, DH = 16, 4, 8
HPG = HEADS // KVH
UNITS = BATCH * KVH
EXPERTS, INTER = 8, 64
HT = (EXPERTS * INTER + 2 * INTER) // P
TILE_ORDER = [HT - 1, *range(HT - 1)]
MT = EXPERTS * INTER // P
EPS = 1e-5
QSCALE = float(DH) ** -0.5

BIAS_ROWS = 15
PROD = 16
RUNS = [(0, 3), (1, 2), (2, 1)]
PARTS = sum(n for _, n in RUNS)
PRODS = DH * PARTS
K1 = 96
WROW = 96
K2 = WROW + 2 * HPG
LOADS = 3
STORES = 2 * len(RUNS)

HALF = 512
QT = HALF // P
STEPS = [(j, kt) for j in range(2) for kt in range(QT * (j + 1))]
NSTEP = len(STEPS)
NEXP = NSTEP * HPG


def pass1_pieces():
    out = []
    for t in range(SEQ // P):
        w = P * (t % QT + 1)
        per = {1: 4, 2: 2, 3: 1, 4: 1}[t % QT + 1]
        for h in range(0, HPG, per):
            out.append((t, h, per, HALF * (t // QT), w, True))
        if t >= QT:
            out += [(t, h, 1, 0, HALF, False) for h in range(HPG)]
    return out


PIECES = pass1_pieces()
NP1 = len(PIECES)
FIRST_HALF = sum(t < QT for t, *_ in PIECES)
PER_STEP = [2, 3, 3, 3, 3, 3, 3, 3, 4, 4, 4, 3]
assert sum(PER_STEP) == NP1 and len(PER_STEP) == NSTEP and NP1 % 2 == 0 and NEXP % 3 == 0
STEP_START = [sum(PER_STEP[:s]) for s in range(NSTEP)]
RING, SBANK, OBANK = 3, 3, 7
START_ITEMS = NP1 + 1
UNIT_ITEMS = NP1 + 4
W1_STEP = 1
OT1_STEP = 2
OT0_STEP = 7
W0_STEP = 9


FFN_SEMS = ("ve", "rs", "xn", "T", "xT", "gl", "lg", "sig", "sel", "mT", "mk", "G", "U", "sg", "h", "tot", "tops",
            "wds", "Y", "yT", "T2", "x", "ch_up", "ch_down", "ve2", "rs2", "xn2", "Tb", "xTb", "Q", "K", "V", "qf",
            "kf", "pt", "v", "dw0", "dw1", "out")
FfnSems = namedtuple("FfnSems", FFN_SEMS)


def after(eng, sem, value):
    if not isinstance(value, int) or value > 0:
        eng.wait_ge(sem, value)


class Chain:

    def __init__(self, eng, sem):
        self.eng, self.sem = eng, sem
        self.base, self.n = 0, 0

    def at(self, base):
        self.base, self.n = base, 0

    def link(self, ins):
        self.n += 1
        ins.then_inc(self.sem, 1)
        self.eng.wait_ge(self.sem, self.base + self.n)


class Ring:

    def __init__(self):
        self.base, self.bank0, self.n = 0, 0, 0

    def unit(self, i, first):
        before = START_ITEMS if first else START_ITEMS - 1 + UNIT_ITEMS * i
        self.base, self.n = before, 0
        self.bank0 = (START_ITEMS if first else START_ITEMS - 1) % RING

    def take(self):
        at = self.bank0 + self.n, self.base + self.n
        self.n += 1
        return at[0] % RING, at[1]


assert UNIT_ITEMS % RING == 0


def over_groups(eng, body):
    body(0, 0, True, False)
    body(1, 1, False, False)
    body(2, 0, False, False)
    with eng.Fori(1, (GROUPS - 2) // 2) as r:
        body(2 * r + 1, 1, False, False)
        body(2 * r + 2, 0, False, False)
    body(GROUPS - 1, 1, False, True)


def over_units(eng, body):
    body(0, 0, True, False)
    with eng.Fori(0, (UNITS - 2) // 2) as r:
        body(2 * r + 1, 1, False, False)
        body(2 * r + 2, 0, False, False)
    body(UNITS - 1, 1, False, True)


def macaron(nc, dram, out):
    ctx = ExitStack()
    with ctx:
        def sb(name, shape, dt=F32):
            return ctx.enter_context(nc.sbuf_tensor(name, shape, dt))

        def sem(name):
            return ctx.enter_context(nc.semaphore(name))

        ps = ctx.enter_context(nc.psum_tensor("ps", [P, 8, 512], F32))

        q_scr = nc.dram_tensor("q_scr", [BATCH, HEADS * DH, PARTS, SEQ], BF16, kind="Internal").ap()
        k_scr = nc.dram_tensor("k_scr", [BATCH, KVH * DH, PARTS, SEQ], BF16, kind="Internal").ap()
        bias_scr = nc.dram_tensor("bias_scr", [HEADS, BIAS_ROWS + 1, SEQ], BF16, kind="Internal").ap()
        q_units = q_scr.rearrange("b (g h d) r n -> (b g) h (d r) n", g=KVH, h=HPG)
        k_units = k_scr.rearrange("b (g d) r n -> (b g) (d r) n", g=KVH)

        c128 = sb("c128", [P, 3 * P + HPG + EXPERTS])
        ident = c128[:, 0:P]
        onehot = c128[:, 3 * P:3 * P + HPG]
        rank = c128[:, 3 * P + HPG:3 * P + HPG + EXPERTS]
        cb = sb("cb", [P, 3 * P], BF16)
        ident_b, mask_qk, mask_kq = cb[:, 0:P], cb[:, P:2 * P], cb[:, 2 * P:3 * P]
        krows = sb("krows", [BIAS_ROWS + 1, SEQ])
        qpos = sb("qpos", [HEADS, SEQ])
        esel_f = sb("esel_f", [EXPERTS, MT * P])
        esel = sb("esel", [EXPERTS, MT * P], BF16)
        ones = sb("ones", [P, P])
        mhalf = sb("mhalf", [P, GT])
        wg = sb("wg", [P, HT, P])
        wu = sb("wu", [P, HT, P])
        wd = sb("wd", [P, HT, P])
        wds = sb("wds", [P, HT, P])
        gate_w = sb("gate_w", [P, EXPERTS])
        lb = sb("lb", [P, EXPERTS])
        wq = sb("wq", [P, P])
        wkv = sb("wkv", [P, 2 * KVH * DH])
        wo = sb("wo", [P, P])
        bq = sb("bq", [P, 1])
        bqs = sb("bqs", [P, 1])
        bk = sb("bk", [KVH * DH, 1])
        bv = sb("bv", [P, KVH * DH])
        bo = sb("bo", [P, P])
        slope = sb("slope", [HEADS, 8])
        sparts = sb("sparts", [HEADS, 3], BF16)

        x = sb("x", [P, TILES, P])
        h_all = sb("h_all", [P, GROUPS, HT, GN])
        stats = sb("stats", [P, GT, 6])
        mv = sb("mv", [P, GT, 2])
        ve = sb("ve", [P, GT])
        rstd = sb("rstd", [P, GT])
        idle = sb("idle", [P, 2])
        xn = sb("xn", [P, GT, P])
        xnT = sb("xnT", [P, 2, GN])
        sg = sb("sg", [P, 2, GN])
        lg = sb("lg", [P, GT, EXPERTS])
        sc = sb("sc", [P, GT, EXPERTS])
        top = sb("top", [P, 8, GT])
        pick = sb("pick", [P, 6, GT, EXPERTS])
        routed = sb("routed", [P, TILES, 2, EXPERTS])
        unsel = sb("unsel", [P, GT, EXPERTS], BF16)
        maskT = sb("maskT", [EXPERTS, 2, GN], BF16)
        tot = sb("tot", [P, 2, EXPERTS])
        wmean = sb("wmean", [P, 3, EXPERTS])
        wrow = sb("wrow", [P, MT])
        yT = sb("yT", [P, 2, GN])

        qf = sb("qf", [P, GN])
        kf = sb("kf", [KVH * DH, GN])
        qres, kres = sg[:, 0, :], sg[0:KVH * DH, 1, :]
        qp = sb("qp", [P, 2, 3, GN], BF16)
        kp = sb("kp", [KVH * DH, 2, 3, GN], BF16)
        v_all = sb("v_all", [P, UNITS, SEQ // P, DH])
        qs = sb("qs", [P, 2, HPG, SEQ], BF16)
        ks = sb("ks", [P, 2, SEQ], BF16)
        vb = sb("vb", [P, 2, SEQ // P, 32])
        mx = sb("mx", [P, 2, 2, QT, HPG])
        mm_ = sb("mm_", [P, QT, HPG])
        wb = sb("wb", [P, QT, 2 * HPG], BF16)
        wt = sb("wt", [P, HALF], BF16)
        osb = sb("osb", [P, 2, HALF])
        rden = sb("rden", [P, QT, HPG])
        attn = sb("attn", [P, UNITS, SEQ // P, HPG * DH])
        pr = h_all[:, 0:3, 0:HPG, :]
        qs_rows = qs[0:HEADS, :, :, :].rearrange("p a h n -> p (a h) n")
        at_rows = attn[0:HEADS, 0:UNITS // 2].rearrange("p u t e -> p (u t e)").bitcast(BF16)\
            .rearrange("p (r n) -> p r n", n=SEQ)
        bias_st = [qs_rows[:, 0:4, :], qs_rows[:, 4:8, :], at_rows]
        bias_f = h_all[0:HEADS, GROUPS - 1, 0:2, :].rearrange("p a n -> p (a n)")
        bias_r = h_all[0:HEADS, GROUPS - 1, 2:4, :].rearrange("p a n -> p (a n)")

        small_loads = [(c128, "c128"), (gate_w, "gate_w"), (lb, "lb"), (esel_f, "esel"), (slope[:, 0:1], "slopes"),
                       (qpos, "qpos")]
        ffn_loads = [(wg, "wg"), (wu, "wu")]
        late_loads = [(wd, "wd"), (krows, "krows"), (bq, "bq"), (bk, "bk"), (bv, "bv"), (bo, "bo"), (wq, "wq"),
                      (wkv, "wkv"), (wo, "wo")]

        s_small = sem("s_small")
        s_w = sem("s_w")
        s_late = sem("s_late")
        s_x0 = sem("s_x0")
        s_init = sem("s_init")
        s_cb = sem("s_cb")
        s_bst = sem("s_bst")
        s_bdma = sem("s_bdma")
        s_dve = sem("s_dve")
        s_zero = sem("s_zero")
        s_kz = sem("s_kz")
        s_ks0 = sem("s_ks0")

        def ffn_sems(n):
            return FfnSems(*[sem(f"f{n}_{name}") for name in FFN_SEMS])

        f1, f2 = ffn_sems(1), ffn_sems(2)
        a_ld = [[sem("a_ld_first_even"), sem("a_ld_first_odd")], [sem("a_ld_second_even"), sem("a_ld_second_odd")]]
        a_vb = sem("a_vb")
        a_in = sem("a_in")
        a_out = sem("a_out")
        a_w = sem("a_w")
        a_wc = sem("a_wc")
        a_wr = sem("a_wr")
        a_sc = sem("a_sc")
        a_ex = sem("a_ex")
        a_pv = sem("a_pv")
        a_ov = sem("a_ov")
        a_on = sem("a_on")
        a_ch = sem("a_ch")
        o_an, o_T, o_aT, o_y, o_x, o_ch = (sem(f"o_{n}") for n in ("an", "T", "aT", "y", "x", "ch"))

        block = ctx.enter_context(nc.Block())

        def xt(c):
            return x[:, bass.ds(c * GT, GT), :]

        def bank(b):
            return ps[:, b, :]

        @block.sync
        def _(sp):
            xd = dram["x"].rearrange("(c t p) f -> c p t f", t=GT, p=P)
            def load(names, s):
                for dst, name in names:
                    sp.dma_start(dst[tuple(slice(None) for _ in dst.shape)], dram[name]).then_inc(s, 16)

            sp.dma_start(x[:, 0:GT, :], xd[0]).then_inc(s_x0, 16)
            load(small_loads, s_small)
            load(ffn_loads, s_w)
            with sp.Fori(1, GROUPS) as c:
                sp.wait_ge(s_x0, 16 * c)
                sp.dma_start(xt(c), xd[c]).then_inc(s_x0, 16)
            load(late_loads, s_late)

            for part in range(3):
                sp.wait_ge(s_bst, part + 1)
                st = bias_st[part]
                for row in (0, 1):
                    sp.dma_start(bias_scr[:, 5 * part + row, :], st[:, 0, :]).then_inc(s_bdma, 16)
                sp.dma_start(bias_scr[:, 5 * part + 2:5 * part + 5, :], st[:, 1:4, :]).then_inc(s_bdma, 16)
            sp.dma_start(bias_scr[:, BIAS_ROWS, :], bias_st[2][:, 3, :]).then_inc(s_bdma, 16)
            sp.wait_ge(s_bdma, 16 * 10)

            def store_parts(c, b, half):
                sp.wait_ge(f1.pt, 2 * c + 2)
                par = half
                n = slice(half * GN, half * GN + GN)
                dw = f1.dw1 if half else f1.dw0
                r = 0
                for part, products in RUNS:
                    sp.dma_start(q_scr[b, :, r:r + products, n],
                                 qp[:, par, part, None, :].broadcast_to([P, products, GN])).then_inc(dw, 16)
                    sp.dma_start(k_scr[b, :, r:r + products, n], kp[:, par, 0:products]).then_inc(dw, 16)
                    r += products

            def load_stack(i, par, g, half):
                s = a_ld[half][par]
                n = slice(half * HALF, half * HALF + HALF)
                sp.dma_start(qs[0:BIAS_ROWS + 1, par, :, n],
                             bias_scr[HPG * g:HPG * g + HPG, :, n].rearrange("h r n -> r h n")).then_inc(s, 16)
                sp.dma_start(ks[PROD:PROD + PRODS, par, n], k_units[i, :, n]).then_inc(s, 16)
                sp.dma_start(qs[PROD:PROD + PRODS, par, :, n],
                             q_units[i, :, :, n].rearrange("h m n -> m h n")).then_inc(s, 16)

            store_parts(0, 0, 0)
            store_parts(1, 0, 1)
            sp.wait_ge(f1.dw0, 16 * STORES)
            sp.wait_ge(f1.dw1, 16 * STORES)
            sp.wait_ge(s_zero, 1)
            sp.wait_ge(s_ks0, 1)
            for half in range(2):
                load_stack(0, 0, 0, half)
            for half in range(2):
                load_stack(1, 1, 1, half)
            with sp.Fori(1, BATCH) as b:
                store_parts(2 * b, b, 0)
                store_parts(2 * b + 1, b, 1)
            sp.wait_ge(f1.dw0, 16 * STORES * BATCH)
            sp.wait_ge(f1.dw1, 16 * STORES * BATCH)

            def reload(i, g):
                sp.wait_ge(a_pv, NSTEP * (i - 2) + 2 * QT)
                load_stack(i, g % 2, g, 0)
                sp.wait_ge(a_pv, NSTEP * (i - 1))
                load_stack(i, g % 2, g, 1)

            reload(2, 2)
            reload(3, 3)
            with sp.Fori(1, BATCH) as b:
                for g in range(KVH):
                    reload(KVH * b + g, g)
            od = out.rearrange("(c t p) f -> c p t f", t=GT, p=P)
            with sp.Fori(0, GROUPS) as c:
                sp.wait_ge(f2.x, c + 1)
                sp.dma_start(od[c], xt(c)).then_inc(f2.out, 16)
            sp.wait_ge(f2.out, 16 * GROUPS)

        @block.gpsimd
        def _(pool):
            pool.memset(mhalf[:, :], -0.5)
            pool.memset(ones[:, :], 1.0)
            pool.memset(vb[:, :, :, :], 0.0).then_inc(s_init, 1)
            pool.wait_ge(s_init, 1)
            pool.memset(vb[:, :, :, DH:DH + 1], 1.0).then_inc(s_init, 1)

            def stack_constants():
                pool.wait_ge(s_init, 2)
                pool.memset(ks[:, :, :], 0.0).then_inc(s_kz, 1)
                pool.wait_ge(s_kz, 1)
                pool.memset(ks[WROW:P, :, :], 1.0)
                pool.memset(qs[64:96, :, :, :], 0.0).then_inc(s_zero, 1)
                pool.wait_ge(s_zero, 1)

            def rsqrt(ve_sem, xn_sem, rs_sem):
                def body(c, par, first, last):
                    pool.wait_ge(ve_sem, c + 1)
                    after(pool, xn_sem, c)
                    pool.tensor_tensor(rstd[:, :], ve[:, :], mhalf[:, :], ALU.pow).then_inc(rs_sem, 1)
                over_groups(pool, body)

            rsqrt(f1.ve, f1.xn, f1.rs)
            stack_constants()
            rsqrt(f1.ve2, f1.xn2, f1.rs2)
            rsqrt(f2.ve, f2.xn, f2.rs)

        @block.scalar
        def _(act):
            copy = ACT.Copy
            act.wait_ge(s_small, 16 * len(small_loads))
            act.activation(cb[:, :], c128[:, 0:3 * P], copy).then_inc(s_cb, 1)
            act.activation(esel[:, :], esel_f[:, :], copy).then_inc(s_cb, 1)

            def stack_constants():
                act.wait_ge(s_late, 16 * len(late_loads))
                act.activation(bqs[:, :], bq[:, :], copy, scale=QSCALE).then_inc(s_cb, 1)
                act.wait_ge(s_zero, 1)
                act.activation(ks[0:BIAS_ROWS + 1, 0, :], krows[:, :], copy)
                act.activation(ks[0:BIAS_ROWS + 1, 1, :], krows[:, :], copy).then_inc(s_ks0, 1)
                act.wait_ge(s_cb, 3)

            def ffn_up(f):
                def xn_T(c, par):
                    act.wait_ge(f.T, c + 1)
                    after(act, f.U, HT * (c - 1))
                    act.activation(xnT[:, par, :], bank(0), copy).then_inc(f.xT, 1)

                def sigmoid(c):
                    act.wait_ge(f.lg, c + 1)
                    after(act, f.sel, c)
                    act.activation(sc[:, :, :], lg[:, :, :], ACT.Sigmoid).then_inc(f.sig, 1)

                def mask_T(c, par):
                    act.wait_ge(f.mT, c + 1)
                    after(act, f.G, HT * (c - 1))
                    act.activation(maskT[:, par, :], ps[0:EXPERTS, 2, 0:GN // 2].bitcast(BF16), copy)\
                       .then_inc(f.mk, 1)

                def silu(c, i, n2):
                    act.wait_ge(f.G, HT * c + i + 1)
                    after(act, f.h, HT * c + i - 1)
                    act.activation(sg[:, n2, :], bank(3 + n2), ACT.Silu).then_inc(f.sg, 1)

                def body(c, par, first, last):
                    for n in range(HT):
                        silu(c, n, (par + n) % 2)
                        if n == 0:
                            mask_T(c, par)
                            if not last:
                                xn_T(c + 1, 1 - par)
                        if n == 1 and not last:
                            sigmoid(c + 1)

                xn_T(0, 0)
                sigmoid(0)
                over_groups(act, body)

            def ffn_down(f, qkv):
                def y_T(c, par):
                    act.wait_ge(f.Y, c + 1)
                    after(act, f.T2, c - 1)
                    act.activation(yT[:, par, :], bank(par), copy).then_inc(f.yT, 1)

                def qk(c):
                    act.wait_ge(f.Q, c + 1)
                    after(act, f.pt, 2 * c)
                    act.activation(qf[:, :], bank(5), ACT.Identity, bias=bqs[:, 0:1], scale=QSCALE)\
                       .then_inc(f.qf, 1)
                    act.wait_ge(f.K, c + 1)
                    act.activation(kf[:, :], ps[0:KVH * DH, 6, :], ACT.Identity, bias=bk[:, 0:1]).then_inc(f.kf, 1)

                def body(c, par, first, last):
                    if qkv and not first:
                        qk(c - 1)
                    if not last:
                        y_T(c + 1, 1 - par)
                    if qkv:
                        act.wait_ge(f.Tb, c + 1)
                        after(act, f.V, c - 1)
                        act.activation(xnT[:, par, :], bank(4), copy).then_inc(f.xTb, 1)

                y_T(0, 0)
                over_groups(act, body)
                if qkv:
                    qk(GROUPS - 1)

            def out_evac(i, j):
                act.wait_ge(a_pv, NSTEP * i + (QT if j == 0 else NSTEP))
                after(act, a_on, 2 * i + j - 1)
                act.activation(osb[:, j, :], bank(OBANK), copy).then_inc(a_ov, 1)

            def attention():
                def body(i, par, first, last):
                    for s, (j, kt) in enumerate(STEPS):
                        lo = max(0, kt - QT * j) * P
                        after(act, a_pv, NSTEP * i + s - 2)
                        for h in range(HPG):
                            m = HPG * s + h
                            act.wait_ge(a_sc, NEXP * i + m + 1)
                            act.activation(pr[:, s % 3, h, lo:HALF], ps[:, SBANK + m % 4, lo:HALF], ACT.Exp)\
                               .then_inc(a_ex, 1)
                        if s == 0 and not first:
                            out_evac(i - 1, 1)
                        if s == QT:
                            out_evac(i, 0)

                over_units(act, body)
                out_evac(UNITS - 1, 1)

            def out_proj():
                def body(c, par, first, last):
                    act.wait_ge(o_T, c + 1)
                    after(act, o_y, c - 1)
                    act.activation(yT[:, par, :], bank(par), copy).then_inc(o_aT, 1)
                over_groups(act, body)

            ffn_up(f1)
            stack_constants()
            ffn_down(f1, True)
            attention()
            out_proj()
            ffn_up(f2)
            ffn_down(f2, False)

        @block.vector
        def _(dve):
            V = ALU

            def slope_parts():
                ch = Chain(dve, s_dve)
                dve.wait_ge(s_small, 16 * len(small_loads))
                for part in range(3):
                    ch.link(dve.tensor_copy(sparts[:, part:part + 1], slope[:, part:part + 1]))
                    if part < 2:
                        ch.link(dve.tensor_tensor(slope[:, part + 1:part + 2], slope[:, part:part + 1],
                                                  sparts[:, part:part + 1], V.subtract))
                    ch.link(dve.tensor_scalar(slope[:, 4 + part:5 + part], sparts[:, part:part + 1], -1.0, None,
                                              V.mult))
                return ch

            def bias_rows(ch, part):
                st = bias_st[part]
                ch.link(dve.tensor_scalar(bias_f, qpos[:, :], slope[:, 4 + part:5 + part], None, V.mult))
                ch.link(dve.tensor_copy(st[:, 1, :], bias_f))
                ch.link(dve.tensor_tensor(bias_r, bias_f, st[:, 1, :], V.subtract))
                ch.link(dve.tensor_copy(st[:, 2, :], bias_r))
                ch.link(dve.tensor_tensor(st[:, 3, :], bias_r, st[:, 2, :], V.subtract))
                dve.tensor_scalar(st[:, 0, :], qpos[:, :], 0.0, slope[:, 4 + part:5 + part],
                                  V.mult, V.subtract).then_inc(s_bst, 1)

            def layer_norm(c, ch, s_ve, s_rs, s_T, s_xn):
                dve.memset(idle[:, 0:1], 0.0)
                for t in range(GT):
                    ins = dve.bn_stats(stats[:, t, :], x[:, c * GT + t, :])
                ch.link(ins)
                dve.memset(idle[:, 1:2], 0.0)
                for t in range(GT):
                    ins = dve.bn_aggr(mv[:, t, :], stats[:, t, :])
                ch.link(ins)
                dve.tensor_scalar(ve[:, :], mv[:, :, 1], EPS, None, V.add).then_inc(s_ve, 1)
                after(dve, s_T, c)
                dve.wait_ge(s_rs, c + 1)
                for t in range(GT):
                    ins = dve.tensor_scalar(xn[:, t, :], x[:, c * GT + t, :], mv[:, t, 0:1], rstd[:, t:t + 1],
                                            V.subtract, V.mult)
                ins.then_inc(s_xn, 1)

            def ffn_up(f, load_sem):
                ch = Chain(dve, f.ch_up)
                LN_LINKS, TOP_LINKS = 2, 17

                def norm(c):
                    ch.at((LN_LINKS + TOP_LINKS) * c)
                    if load_sem is not None:
                        dve.wait_ge(load_sem, 16 * c + 16)
                    layer_norm(c, ch, f.ve, f.rs, f.T, f.xn)

                def logits(c):
                    dve.wait_ge(f.gl, c + 1)
                    dve.tensor_tensor(lg[:, :, :], ps[:, 1, 0:GT * EXPERTS].rearrange("p (t e) -> p t e", t=GT),
                                      lb[:, None, :].broadcast_to([P, GT, EXPERTS]), V.add).then_inc(f.lg, 1)

                rk = rank[:, None, :].broadcast_to([P, GT, EXPERTS])
                pick1, pick2, s2, eq, wt = (pick[:, n] for n in range(5))
                m1, m2, r1, r2, den, w1, w2 = (top[:, n] for n in range(7))

                def wide(a):
                    return a[:, :, None].broadcast_to([P, GT, EXPERTS])

                def first_max(scores, m, r, sel):
                    ch.link(dve.tensor_reduce(m, scores, AX.X, V.max))
                    ch.link(dve.tensor_tensor(eq, scores, wide(m), V.is_equal))
                    ch.link(dve.tensor_tensor(eq, eq, rk, V.mult))
                    ch.link(dve.tensor_reduce(r, eq, AX.X, V.max))
                    ch.link(dve.tensor_tensor(sel, rk, wide(r), V.is_equal))

                def top1(c):
                    ch.at((LN_LINKS + TOP_LINKS) * c + LN_LINKS)
                    dve.wait_ge(f.sig, c + 1)
                    first_max(sc[:, :, :], m1, r1, pick1)

                def top2(c):
                    ch.link(dve.scalar_tensor_tensor(out=s2, in0=pick1, scalar=-4.0, in1=sc[:, :, :],
                                                     op0=V.mult, op1=V.add))
                    first_max(s2, m2, r2, pick2)
                    after(dve, f.mT, c)
                    dve.scalar_tensor_tensor(out=unsel[:, :, :], in0=pick1, scalar=-1.0, in1=pick2,
                                             op0=V.add, op1=V.add).then_inc(f.sel, 1)

                def weights(c):
                    dve.tensor_tensor(routed[:, bass.ds(c * GT, GT), 1, :], pick1, pick2, V.add)
                    ch.link(dve.tensor_tensor(den, m1, m2, V.add))
                    ch.link(dve.tensor_scalar(den, den, 1e-8, None, V.add))
                    ch.link(dve.reciprocal(den, den))
                    dve.tensor_tensor(w1, m1, den, V.mult)
                    ch.link(dve.tensor_tensor(w2, m2, den, V.mult))
                    dve.tensor_tensor(wt, pick1, wide(w1), V.mult)
                    ch.link(dve.tensor_tensor(s2, pick2, wide(w2), V.mult))
                    ch.link(dve.tensor_tensor(routed[:, bass.ds(c * GT, GT), 0, :], wt, s2, V.add))
                    assert ch.n == TOP_LINKS, ch.n

                def hidden(c, n, tile, n2):
                    dve.wait_ge(f.U, HT * c + n + 1)
                    dve.wait_ge(f.sg, HT * c + n + 1)
                    dve.tensor_tensor(h_all[:, c, tile, :], bank(5 + n2), sg[:, n2, :], V.mult).then_inc(f.h, 1)

                def body(c, par, first, last):
                    if not last:
                        norm(c + 1)
                    for n, tile in enumerate(TILE_ORDER):
                        hidden(c, n, tile, (par + n) % 2)
                        if n and not last:
                            (logits, top1, top2, weights)[n - 1](c + 1)
                    if load_sem is not None and isinstance(c, int) and c < 3:
                        bias_rows(slopes, c)

                norm(0)
                logits(0)
                top1(0)
                top2(0)
                weights(0)
                over_groups(dve, body)
                ch.at((LN_LINKS + TOP_LINKS) * GROUPS)
                dve.tensor_reduce(tot[:, :, :], routed[:, :, :, :].rearrange("p t w e -> p w e t"), AX.X, V.add)\
                   .then_inc(f.tot, 1)
                dve.wait_ge(f.tops, 1)
                dve.wait_ge(s_late, 16 * len(late_loads))
                t2 = ps[:, 1, 0:2 * EXPERTS].rearrange("p (w e) -> p w e", w=2)
                ch.link(dve.tensor_scalar(wmean[:, 1, :], t2[:, 1, :], 1.0, None, V.max))
                ch.link(dve.reciprocal(wmean[:, 2, :], wmean[:, 1, :]))
                ch.link(dve.scalar_tensor_tensor(out=wmean[:, 0, :], in0=t2[:, 0, :], scalar=0.5,
                                                 in1=wmean[:, 2, :], op0=V.mult, op1=V.mult))
                for k in range(2):
                    rows = slice(k * INTER, k * INTER + INTER)
                    ins = dve.tensor_copy(wrow[rows, :], wmean[rows, 0, k:EXPERTS:2])
                ch.link(ins)
                for i in range(MT):
                    dve.tensor_scalar(wds[:, i, :], wd[:, i, :], wrow[:, i:i + 1], None, V.mult)
                dve.tensor_scalar(wds[:, MT, :], wd[:, MT, :], 0.5, None, V.mult).then_inc(f.wds, 1)

            def ffn_down(f, qkv):
                ch = Chain(dve, f.ch_down)
                LN_LINKS, SPLIT_LINKS = 2, 6
                LINKS = LN_LINKS + SPLIT_LINKS

                def split(src, rest, parts, done, ready, c):
                    dve.wait_ge(ready, c + 1)
                    ch.link(dve.tensor_copy(parts[:, 0, :], src))
                    ch.link(dve.tensor_tensor(rest, src, parts[:, 0, :], V.subtract))
                    ch.link(dve.tensor_copy(parts[:, 1, :], rest))
                    dve.tensor_tensor(parts[:, 2, :], rest, parts[:, 1, :], V.subtract).then_inc(done, 1)

                def projections(c, par, tail=False):
                    after(dve, f.dw1 if par else f.dw0, 8 * STORES * (c - par))
                    split(qf[:, :], qres, qp[:, par], f.pt, f.qf, c)
                    split(kf[:, :], kres, kp[:, par], f.pt, f.kf, c)
                    dve.wait_ge(f.V, c + 1)

                def values(c, b, half):
                    vin = ps[:, 7, 0:GT * KVH * DH].rearrange("p (t g d) -> p g t d", t=GT, g=KVH)
                    vout = v_all[:, bass.ds(KVH * b, KVH), GT * half:GT * half + GT, :]
                    for t in range(GT):
                        ins = dve.tensor_tensor(vout[:, :, t, :], vin[:, :, t, :],
                                                bv[:, :].rearrange("p (g d) -> p g d", g=KVH), V.add)
                    ins.then_inc(f.v, 1)

                def body(c, par, first, last, b=None):
                    dve.wait_ge(f.T2, c + 1)
                    ins = dve.tensor_tensor(xt(c), xt(c),
                                            bank(2 + par).rearrange("p (t f) -> p t f", t=GT), V.add)
                    ins.then_inc(f.x, 1)
                    if qkv:
                        ch.at(0 if first else LINKS * c - SPLIT_LINKS)
                        dve.wait_ge(f.x, c + 1)
                        layer_norm(c, ch, f.ve2, f.rs2, f.Tb, f.xn2)
                        if not first:
                            prev(c, par)

                def prev(c, par):
                    projections(c - 1, 1 - par)

                if not qkv:
                    over_groups(dve, body)
                    return
                body(0, 0, True, False)
                body(1, 1, False, False)
                values(0, 0, 0)
                body(2, 0, False, False)
                values(1, 0, 1)
                with dve.Fori(1, (GROUPS - 2) // 2) as r:
                    body(2 * r + 1, 1, False, False)
                    values(2 * r, r, 0)
                    body(2 * r + 2, 0, False, False)
                    values(2 * r + 1, r, 1)
                body(GROUPS - 1, 1, False, True)
                values(GROUPS - 2, BATCH - 1, 0)
                ch.at(LINKS * GROUPS - SPLIT_LINKS)
                projections(GROUPS - 1, 1)
                values(GROUPS - 1, BATCH - 1, 1)

            def attention():
                ch = Chain(dve, a_ch)

                def load_v(i, par):
                    after(dve, a_pv, NSTEP * (i - 1))
                    dve.tensor_copy(vb[:, par, :, 0:DH], v_all[:, i, :, :]).then_inc(a_vb, 1)

                ring = Ring()

                def reduce(n):
                    t, h, per, k0, w, diag = PIECES[n]
                    b, done = ring.take()
                    dve.wait_ge(a_in, done + 1)
                    src = ps[:, b, 0:per * w].rearrange("p (h w) -> p h w", h=per)
                    dve.tensor_reduce(mx[:, t // QT, 0 if diag else 1, t % QT, h:h + per], src, AX.X, V.max)\
                       .then_inc(a_out, 1)
                    return done + 1

                def rows_out(i, par, j):
                    b, done = ring.take()
                    dve.wait_ge(a_in, done + 1)
                    after(dve, a_wr, 2 * i + j)
                    dve.tensor_copy(wt[WROW:K2, :], ps[WROW:K2, b, 0:HALF // 2].bitcast(BF16)).then_inc(a_wc, 1)
                    dve.wait_ge(a_wc, 2 * i + j + 1)
                    dve.memset(idle[:, 0:1], 0.0).then_inc(a_out, 1)
                    for h in range(HPG):
                        ins = dve.tensor_scalar(qs[WROW:K2, par, h, HALF * j:HALF * j + HALF], wt[WROW:K2, :],
                                                onehot[WROW:K2, h:h + 1], None, V.mult)
                    ins.then_inc(a_wr, 1)

                def maxima(i, j, done):
                    dve.wait_ge(a_out, done)
                    m = mx[:, 0, 0]
                    if j:
                        m = mm_[:, :, :]
                        ch.link(dve.tensor_tensor(m, mx[:, 1, 0], mx[:, 1, 1], V.max))
                    after(dve, a_wc, 2 * i + j)
                    ch.link(dve.tensor_scalar(wb[:, :, 0:HPG], m, -1.0, None, V.mult))
                    dve.scalar_tensor_tensor(out=wb[:, :, HPG:2 * HPG], in0=m, scalar=-1.0, in1=wb[:, :, 0:HPG],
                                             op0=V.mult, op1=V.subtract).then_inc(a_w, 1)

                def normalise(i, j):
                    b, done = ring.take()
                    after(dve, a_on, 2 * i + j)
                    dve.wait_ge(a_in, done + 1)
                    o = bank(b).rearrange("p (t h e) -> p t h e", t=QT, h=HPG)
                    ch.link(dve.reciprocal(rden[:, :, :], o[:, :, :, DH]))
                    for t in range(QT):
                        ins = dve.tensor_tensor(
                            attn[:, i, QT * j + t, :].rearrange("p (h d) -> p h d", h=HPG), o[:, t, :, 0:DH],
                            rden[:, t, :, None].broadcast_to([P, HPG, DH]), V.mult)
                    ins.then_inc(a_on, 1)
                    dve.wait_ge(a_on, 2 * i + j + 1)
                    dve.memset(idle[:, 0:1], 0.0).then_inc(a_out, 1)

                load_v(0, 0)
                for n in range(NP1):
                    done = reduce(n)
                    if n == FIRST_HALF - 1:
                        maxima(0, 0, done)
                rows_out(0, 0, 0)
                maxima(0, 1, done)
                START_LINKS = 3
                UNIT_LINKS = 2 + 3

                def body(i, par, first, last):
                    ch.at(START_LINKS + UNIT_LINKS * i - (0 if first else 1))
                    ring.unit(i, first)
                    if not last:
                        load_v(i + 1, 1 - par)
                    for s in range(NSTEP):
                        if not last:
                            for n in range(STEP_START[s], STEP_START[s] + PER_STEP[s]):
                                done = reduce(n)
                                if n == FIRST_HALF - 1:
                                    maxima(i + 1, 0, done)
                        if s == W1_STEP:
                            rows_out(i, par, 1)
                        if s == OT1_STEP and not first:
                            normalise(i - 1, 1)
                        if s == OT0_STEP:
                            normalise(i, 0)
                        if s == W0_STEP and not last:
                            rows_out(i + 1, 1 - par, 0)
                    if not last:
                        maxima(i + 1, 1, done)

                over_units(dve, body)
                normalise(UNITS - 1, 1)

            def out_proj():
                ch = Chain(dve, o_ch)

                def gather(c, b, half, par):
                    after(dve, o_T, c - 1)
                    src = attn[:, bass.ds(KVH * b, KVH), GT * half:GT * half + GT, :]
                    dst = sg[:, par, :].rearrange("p (t g e) -> p g t e", t=GT, g=KVH)
                    for t in range(GT):
                        ins = dve.tensor_copy(dst[:, :, t, :], src[:, :, t, :])
                    ins.then_inc(o_an, 1)

                def residual(c, par):
                    ch.at(c)
                    dve.wait_ge(o_y, c + 1)
                    ch.link(dve.tensor_tensor(xt(c), xt(c), bank(2 + par).rearrange("p (t f) -> p t f", t=GT), V.add))
                    dve.tensor_tensor(xt(c), xt(c), bo[:, None, :].broadcast_to([P, GT, P]), V.add).then_inc(o_x, 1)

                dve.wait_ge(a_on, 2 * UNITS)
                gather(0, 0, 0, 0)
                gather(1, 0, 1, 1)
                with dve.Fori(0, BATCH - 1) as b:
                    residual(2 * b, 0)
                    gather(2 * b + 2, b + 1, 0, 0)
                    residual(2 * b + 1, 1)
                    gather(2 * b + 3, b + 1, 1, 1)
                residual(GROUPS - 2, 0)
                residual(GROUPS - 1, 1)
                dve.wait_ge(o_x, GROUPS)

            slopes = slope_parts()
            ffn_up(f1, s_x0)
            ffn_down(f1, True)
            attention()
            out_proj()
            ffn_up(f2, None)
            ffn_down(f2, False)

        @block.tensor
        def _(pe):
            def mm(o, l, r, start=True, stop=True):
                return pe.matmul(o, l, r, start=start, stop=stop, skip_group_check=True)

            def turn(src, b):
                for t in range(GT):
                    ins = pe.transpose(ps[:, b, t * P:(t + 1) * P], src(t), ident)
                return ins

            def ffn_up(f):
                def xn_T(c):
                    pe.wait_ge(f.xn, c + 1)
                    after(pe, f.xT, c)
                    turn(lambda t: xn[:, t, :], 0).then_inc(f.T, 1)

                def gate(c, par):
                    pe.wait_ge(f.xT, c + 1)
                    after(pe, f.lg, c)
                    for t in range(GT):
                        ins = mm(ps[:, 1, EXPERTS * t:EXPERTS * t + EXPERTS], xnT[:, par, t * P:(t + 1) * P],
                                 gate_w[:, :])
                    ins.then_inc(f.gl, 1)

                def mask_T(c):
                    pe.wait_ge(f.sel, c + 1)
                    after(pe, f.mk, c)
                    o = ps[0:EXPERTS, 2, 0:GN // 2].bitcast(BF16)
                    for t in range(GT):
                        ins = pe.transpose(o[:, t * P:(t + 1) * P], unsel[:, t, :], ident_b)
                    ins.then_inc(f.mT, 1)

                def up(c, n, tile, n2, par):
                    after(pe, f.sg, HT * c + n - 1)
                    routed_tile = tile < MT
                    ins = mm(bank(3 + n2), wg[:, tile, :], xnT[:, par, :], stop=not routed_tile)
                    if routed_tile:
                        ins = mm(bank(3 + n2), esel[:, tile * P:(tile + 1) * P], maskT[:, par, :], start=False)
                    ins.then_inc(f.G, 1)
                    after(pe, f.h, HT * c + n - 1)
                    mm(bank(5 + n2), wu[:, tile, :], xnT[:, par, :]).then_inc(f.U, 1)

                def body(c, par, first, last):
                    for n, tile in enumerate(TILE_ORDER):
                        if n == 1:
                            pe.wait_ge(f.mk, c + 1)
                        up(c, n, tile, (par + n) % 2, par)
                        if n == 0:
                            mask_T(c)
                            if not last:
                                xn_T(c + 1)
                        if n == 1 and not last:
                            gate(c + 1, 1 - par)

                xn_T(0)
                gate(0, 0)
                pe.wait_ge(s_w, 16 * len(ffn_loads))
                over_groups(pe, body)
                pe.wait_ge(f.tot, 1)
                mm(ps[:, 1, 0:2 * EXPERTS], ones[:, :], tot[:, :, :].rearrange("p w e -> p (w e)"))\
                    .then_inc(f.tops, 1)

            def ffn_down(f, qkv):
                def down(c, par):
                    after(pe, f.yT, c - 1)
                    for i in range(HT):
                        ins = mm(bank(par), wds[:, i, :], h_all[:, c, i, :], start=(i == 0), stop=(i == HT - 1))
                    ins.then_inc(f.Y, 1)

                def project(c, par):
                    pe.wait_ge(f.xTb, c + 1)
                    after(pe, f.qf, c)
                    mm(bank(5), wq[:, :], xnT[:, par, :]).then_inc(f.Q, 1)
                    after(pe, f.kf, c)
                    mm(ps[0:KVH * DH, 6, :], wkv[:, 0:KVH * DH], xnT[:, par, :]).then_inc(f.K, 1)
                    after(pe, f.v, c)
                    w = KVH * DH
                    for t in range(GT):
                        ins = mm(ps[:, 7, w * t:w * t + w], xnT[:, par, t * P:(t + 1) * P], wkv[:, w:2 * w])
                    ins.then_inc(f.V, 1)

                def body(c, par, first, last):
                    pe.wait_ge(f.yT, c + 1)
                    after(pe, f.x, c - 1)
                    turn(lambda t: yT[:, par, t * P:(t + 1) * P], 2 + par).then_inc(f.T2, 1)
                    if qkv and not first:
                        project(c - 1, 1 - par)
                    if not last:
                        down(c + 1, 1 - par)
                    if qkv:
                        pe.wait_ge(f.xn2, c + 1)
                        after(pe, f.xTb, c)
                        turn(lambda t: xn[:, t, :], 4).then_inc(f.Tb, 1)

                pe.wait_ge(f.wds, 1)
                down(0, 0)
                over_groups(pe, body)
                if qkv:
                    project(GROUPS - 1, 1)

            ring = Ring()

            def slot():
                b, done = ring.take()
                after(pe, a_out, done - RING + 1)
                return b

            def piece(n, par):
                t, h0, per, k0, w, diag = PIECES[n]
                b = slot()
                for k in range(per):
                    ins = mm(ps[:, b, k * w:k * w + w], qs[0:K1, par, h0 + k, t * P:(t + 1) * P],
                             ks[0:K1, par, k0:k0 + w], stop=not diag)
                    if diag:
                        ins = mm(ps[:, b, k * w + w - P:k * w + w], ident_b, mask_qk, start=False)
                ins.then_inc(a_in, 1)

            def maxima_T(i, j):
                b = slot()
                pe.wait_ge(a_w, 2 * i + j + 1)
                o = ps[WROW:K2, b, 0:HALF // 2].bitcast(BF16)
                for t in range(QT):
                    ins = pe.transpose(o[:, t * P:(t + 1) * P], wb[:, t, :], ident_b)
                ins.then_inc(a_in, 1)

            def out_T(i, j):
                b = slot()
                pe.wait_ge(a_ov, 2 * i + j + 1)
                turn(lambda t: osb[:, j, t * P:(t + 1) * P], b).then_inc(a_in, 1)

            def score(i, s, h, par):
                j, kt = STEPS[s]
                m = HPG * s + h
                lo = max(0, kt - QT * j) * P
                diag = kt >= QT * j
                after(pe, a_ex, NEXP * i + m - 3)
                b = SBANK + m % 4
                ins = mm(ps[:, b, lo:HALF], ks[0:K2, par, kt * P:(kt + 1) * P],
                         qs[0:K2, par, h, HALF * j + lo:HALF * j + HALF], stop=not diag)
                if diag:
                    ins = mm(ps[:, b, lo:lo + P], ident_b, mask_kq, start=False)
                ins.then_inc(a_sc, 1)

            def times_v(i, s, par):
                j, kt = STEPS[s]
                lo = max(0, kt - QT * j) * P
                last = kt == QT * (j + 1) - 1
                pe.wait_ge(a_ex, NEXP * i + HPG * (s + 1))
                if kt == 0:
                    after(pe, a_ov, 2 * i + j)
                for h in range(HPG):
                    ins = mm(ps[32 * h:32 * h + 32, OBANK, lo:HALF], vb[:, par, kt, :], pr[:, s % 3, h, lo:HALF],
                             start=(kt == 0), stop=last)
                ins.then_inc(a_pv, 1)

            def attention():
                def next_stack(i, par, half):
                    pe.wait_ge(a_ld[half][1 - par], 8 * LOADS * (i + 3 if par else i + 2))

                for half in range(2):
                    pe.wait_ge(a_ld[half][0], 16 * LOADS)
                for n in range(NP1):
                    piece(n, 0)
                maxima_T(0, 0)
                pe.wait_ge(a_wr, 1)
                for h in range(HPG):
                    score(0, 0, h, 0)

                def body(i, par, first, last):
                    ring.unit(i, first)
                    pe.wait_ge(a_vb, i + 1)
                    for s in range(NSTEP):
                        todo = [] if last else list(range(STEP_START[s], STEP_START[s] + PER_STEP[s]))
                        if s + 1 == QT:
                            pe.wait_ge(a_wr, 2 * i + 2)
                        if s + 1 == NSTEP and not last:
                            pe.wait_ge(a_wr, 2 * i + 3)
                        if 0 in todo:
                            next_stack(i, par, 0)
                        for h in range(HPG):
                            if h < len(todo) and todo[h] == FIRST_HALF:
                                next_stack(i, par, 1)
                            if s + 1 < NSTEP:
                                score(i, s + 1, h, par)
                            elif not last:
                                score(i + 1, 0, h, 1 - par)
                            if h < len(todo):
                                piece(todo[h], 1 - par)
                        times_v(i, s, par)
                        if s == W1_STEP:
                            maxima_T(i, 1)
                        if s == OT1_STEP and not first:
                            out_T(i - 1, 1)
                        if s == OT0_STEP:
                            out_T(i, 0)
                        if s == W0_STEP and not last:
                            maxima_T(i + 1, 0)

                over_units(pe, body)
                out_T(UNITS - 1, 1)

            def out_proj():
                def body(c, par, first, last):
                    pe.wait_ge(o_an, c + 1)
                    after(pe, o_aT, c - 1)
                    turn(lambda t: sg[:, par, t * P:(t + 1) * P], par).then_inc(o_T, 1)
                    pe.wait_ge(o_aT, c + 1)
                    after(pe, o_x, c - 1)
                    for t in range(GT):
                        ins = mm(ps[:, 2 + par, t * P:(t + 1) * P], yT[:, par, t * P:(t + 1) * P], wo[:, :])
                    ins.then_inc(o_y, 1)
                over_groups(pe, body)

            pe.wait_ge(s_small, 16 * len(small_loads))
            pe.wait_ge(s_cb, 2)
            pe.wait_ge(s_init, 2)
            ffn_up(f1)
            pe.wait_ge(s_late, 16 * len(late_loads))
            ffn_down(f1, True)
            attention()
            out_proj()
            ffn_up(f2)
            ffn_down(f2, False)


def kernel(L0_attn_qkv, L0_attn_Wq, L0_attn_bq, L0_attn_Wk, L0_attn_bk, L0_attn_Wv, L0_attn_bv, L0_attn_Wo,
           L0_attn_bo, L0_attn_slopes, L0_ffn_gate_w, L0_ffn_lb_bias, L0_ffn_expert_gate_w, L0_ffn_expert_up_w,
           L0_ffn_expert_down_w, L0_ffn_shared_gate_w, L0_ffn_shared_up_w, L0_ffn_shared_down_w):
    import numpy as np
    import concourse.bacc as bacc
    from concourse.bass_utils import run_bass_kernel_spmd

    def arr(a):
        return np.ascontiguousarray(np.asarray(a))

    at = np.arange(P)
    c128 = np.zeros((P, 3 * P + HPG + EXPERTS), np.float32)
    c128[:, 0:P] = np.eye(P)
    c128[:, P:2 * P] = np.where(at[None, :] > at[:, None], -1e30, 0.0)
    c128[:, 2 * P:3 * P] = np.where(at[:, None] > at[None, :], -1e30, 0.0)
    for h in range(HPG):
        c128[[WROW + h, WROW + HPG + h], 3 * P + h] = 1.0
    c128[:, 3 * P + HPG:] = np.arange(EXPERTS, 0, -1)
    pos = np.arange(SEQ, dtype=np.float32)
    krows = np.zeros((BIAS_ROWS + 1, SEQ), np.float32)
    for part in range(3):
        krows[5 * part] = pos - pos % 8
        krows[5 * part + 1] = pos % 8
        krows[5 * part + 2:5 * part + 5] = 1.0
    esel = np.zeros((EXPERTS, MT, P), np.float32)
    for e in range(EXPERTS):
        esel[e, e // 2, (e % 2) * INTER:(e % 2) * INTER + INTER] = 2.0 ** 30

    def up(experts, shared):
        w = np.concatenate([arr(experts).reshape(EXPERTS * INTER, DM), arr(shared)], 0)
        return arr(w.T.reshape(DM, HT, P))

    down = np.concatenate([arr(L0_ffn_expert_down_w).transpose(0, 2, 1).reshape(EXPERTS * INTER, DM),
                           arr(L0_ffn_shared_down_w).T], 0)
    data = {
        "x": arr(L0_attn_qkv).reshape(BATCH * SEQ, DM),
        "slopes": arr(L0_attn_slopes).reshape(HEADS, 1),
        "c128": c128, "krows": krows, "qpos": arr(np.broadcast_to(pos, (HEADS, SEQ))),
        "esel": esel.reshape(EXPERTS, MT * P),
        "gate_w": arr(arr(L0_ffn_gate_w).T),
        "lb": arr(np.broadcast_to(arr(L0_ffn_lb_bias), (P, EXPERTS))),
        "bq": arr(L0_attn_bq).reshape(DM, 1), "bk": arr(L0_attn_bk).reshape(KVH * DH, 1),
        "bv": arr(np.broadcast_to(arr(L0_attn_bv), (P, KVH * DH))),
        "bo": arr(np.broadcast_to(arr(L0_attn_bo), (P, DM))),
        "wg": up(L0_ffn_expert_gate_w, L0_ffn_shared_gate_w),
        "wu": up(L0_ffn_expert_up_w, L0_ffn_shared_up_w),
        "wd": arr(down.reshape(HT, P, DM).transpose(1, 0, 2)),
        "wq": arr(L0_attn_Wq), "wkv": arr(np.concatenate([arr(L0_attn_Wk), arr(L0_attn_Wv)], 1)),
        "wo": arr(L0_attn_Wo),
    }
    nc = bacc.Bacc("TRN2", target_bir_lowering=False, num_devices=1)
    dram = {n: nc.dram_tensor(f"in_{n}", a.shape, F32, kind="ExternalInput").ap() for n, a in data.items()}
    out = nc.dram_tensor("out", (BATCH * SEQ, DM), F32, kind="ExternalOutput").ap()
    macaron(nc, dram, out)
    r = run_bass_kernel_spmd(nc, [{f"in_{n}": a for n, a in data.items()}], core_ids=[0])
    return r.results[0]["out"].reshape(BATCH, SEQ, DM)
```

```python
from collections import namedtuple
from contextlib import ExitStack

import concourse.bass as bass
from concourse import mybir

F32 = mybir.dt.float32
BF16 = mybir.dt.bfloat16
ALU = mybir.AluOpType
ACT = mybir.ActivationFunctionType
AX = mybir.AxisListType

P = 128
BATCH, SEQ, DM = 4, 1024, 128
TILES = BATCH * SEQ // P
GT = 4
GN = GT * P
GROUPS = TILES // GT
HEADS, KVH, DH = 16, 4, 8
HPG = HEADS // KVH
UNITS = BATCH * KVH
EXPERTS, INTER = 8, 64
HT = (EXPERTS * INTER + 2 * INTER) // P
MT = EXPERTS * INTER // P
EPS = 1e-5
LOWEST = -3e38
QSCALE = float(DH) ** -0.5

BIAS_ROWS = 15
PROD = 16
RUNS = [(0, 3), (1, 2), (2, 1)]
PARTS = sum(n for _, n in RUNS)
PRODS = DH * PARTS
K1 = 96
WROW = 96
K2 = WROW + 2 * HPG
LOADS = 3
STORES = 2 * len(RUNS)

HALF = 512
QT = HALF // P
STEPS = [(j, kt) for j in range(2) for kt in range(QT * (j + 1))]
NSTEP = len(STEPS)
NEXP = NSTEP * HPG


def pass1_pieces():
    out = []
    for t in range(SEQ // P):
        w = P * (t % QT + 1)
        per = {1: 4, 2: 2, 3: 1, 4: 1}[t % QT + 1]
        for h in range(0, HPG, per):
            out.append((t, h, per, HALF * (t // QT), w, True))
        if t >= QT:
            out += [(t, h, 1, 0, HALF, False) for h in range(HPG)]
    return out


PIECES = pass1_pieces()
NP1 = len(PIECES)
FIRST_HALF = sum(t < QT for t, *_ in PIECES)
PER_STEP = [4, 3, 2, 2, 4, 4, 4, 4, 4, 4, 2, 1]
assert sum(PER_STEP) == NP1 and len(PER_STEP) == NSTEP and NP1 % 2 == 0 and NEXP % 3 == 0
STEP_START = [sum(PER_STEP[:s]) for s in range(NSTEP)]
RING, SBANK, OBANK = 3, 3, 7
START_ITEMS = NP1 + 1
UNIT_ITEMS = NP1 + 4
POOL_HEADS = [range(HPG), range(HPG // 2, HPG)]
EARLY = [range(0, 3), range(3, 9), range(9, 11)]
START_T = EARLY[2][-1] + 4
W1_STEP = 0
OT1_STEP = 2
OT0_STEP = 7
W0_STEP = 6


FFN_SEMS = ("ve", "rs", "xn", "T", "xT", "xA", "gl", "lg", "sig", "sel", "mT", "mk", "G", "U", "sg", "h", "tot", "tops",
            "wds", "Y", "yT", "T2", "x", "ch_up", "ch_down", "ve2", "rs2", "xn2", "Tb", "xTb", "Q", "K", "V", "qf", "k0",
            "kf", "pq", "pk", "ch_k", "v", "dw0", "dw1", "out")
FfnSems = namedtuple("FfnSems", FFN_SEMS)


def after(eng, sem, value):
    if not isinstance(value, int) or value > 0:
        eng.wait_ge(sem, value)


class Chain:

    def __init__(self, eng, sem):
        self.eng, self.sem = eng, sem
        self.base, self.n = 0, 0

    def at(self, base):
        self.base, self.n = base, 0

    def link(self, ins):
        self.n += 1
        ins.then_inc(self.sem, 1)
        self.eng.wait_ge(self.sem, self.base + self.n)


class Ring:

    def __init__(self):
        self.base, self.bank0, self.n = 0, 0, 0

    def unit(self, i, first):
        before = START_ITEMS if first else START_ITEMS - 1 + UNIT_ITEMS * i
        self.base, self.n = before, 0
        self.bank0 = (START_ITEMS if first else START_ITEMS - 1) % RING

    def take(self):
        at = self.bank0 + self.n, self.base + self.n
        self.n += 1
        return at[0] % RING, at[1]


assert UNIT_ITEMS % RING == 0


def over_groups(eng, body):
    body(0, 0, True, False)
    body(1, 1, False, False)
    body(2, 0, False, False)
    with eng.Fori(1, (GROUPS - 2) // 2) as r:
        body(2 * r + 1, 1, False, False)
        body(2 * r + 2, 0, False, False)
    body(GROUPS - 1, 1, False, True)


def over_units(eng, body):
    body(0, 0, True, False)
    with eng.Fori(0, (UNITS - 2) // 2) as r:
        body(2 * r + 1, 1, False, False)
        body(2 * r + 2, 0, False, False)
    body(UNITS - 1, 1, False, True)


def macaron(nc, dram, out):
    ctx = ExitStack()
    with ctx:
        def sb(name, shape, dt=F32):
            return ctx.enter_context(nc.sbuf_tensor(name, shape, dt))

        def sem(name):
            return ctx.enter_context(nc.semaphore(name))

        ps = ctx.enter_context(nc.psum_tensor("ps", [P, 8, 512], F32))

        q_scr = nc.dram_tensor("q_scr", [BATCH, HEADS * DH, PARTS, SEQ], BF16, kind="Internal").ap()
        k_scr = nc.dram_tensor("k_scr", [BATCH, KVH * DH, PARTS, SEQ], BF16, kind="Internal").ap()
        bias_scr = nc.dram_tensor("bias_scr", [HEADS, BIAS_ROWS + 1, SEQ], BF16, kind="Internal").ap()
        q_units = q_scr.rearrange("b (g h d) r n -> (b g) h (d r) n", g=KVH, h=HPG)
        k_units = k_scr.rearrange("b (g d) r n -> (b g) (d r) n", g=KVH)

        c128 = sb("c128", [P, 3 * P + HPG + EXPERTS])
        ident = c128[:, 0:P]
        mask_w = sb("mask_w", [P, HALF])
        onehot = c128[:, 3 * P:3 * P + HPG]
        rank = c128[:, 3 * P + HPG:3 * P + HPG + EXPERTS]
        cb = sb("cb", [P, 3 * P], BF16)
        ident_b, mask_qk, mask_kq = cb[:, 0:P], cb[:, P:2 * P], cb[:, 2 * P:3 * P]
        krows = sb("krows", [BIAS_ROWS + 1, SEQ])
        qpos = sb("qpos", [HEADS, SEQ])
        esel_f = sb("esel_f", [EXPERTS, MT * P])
        esel = sb("esel", [EXPERTS, MT * P], BF16)
        ones = sb("ones", [P, P])
        mhalf = sb("mhalf", [P, GT])
        wg = sb("wg", [P, HT, P])
        wu = sb("wu", [P, HT, P])
        wd = sb("wd", [P, HT, P])
        wds = sb("wds", [P, HT, P])
        gate_w = sb("gate_w", [P, EXPERTS])
        lb = sb("lb", [P, EXPERTS])
        wq = sb("wq", [P, P])
        wkv = sb("wkv", [P, 2 * KVH * DH])
        wo = sb("wo", [P, P])
        bq = sb("bq", [P, 1])
        bqs = sb("bqs", [P, 1])
        bkv = sb("bkv", [2 * KVH * DH, 1])
        bo = sb("bo", [P, P])
        slope = sb("slope", [HEADS, 8])
        sparts = sb("sparts", [HEADS, 3], BF16)

        x = sb("x", [P, TILES, P])
        h_all = sb("h_all", [P, GROUPS, HT, GN])
        stats = sb("stats", [P, 2, GT, 6])
        mv = sb("mv", [P, 2, GT, 2])
        ve = sb("ve", [P, 2, GT])
        rstd = sb("rstd", [P, 2, GT])
        idle = sb("idle", [P, 4 + HPG])
        xn = sb("xn", [P, GT, P])
        xnT = sb("xnT", [P, 2, GN])
        sg = sb("sg", [P, 2, GN])
        routed = sb("routed", [P, TILES, 2, EXPERTS])
        unsel = sb("unsel", [P, TILES, EXPERTS], BF16)
        unsel_g = sb("unsel_g", [P, 2, GT, EXPERTS], BF16)
        maskT = sb("maskT", [EXPERTS, 2, GN], BF16)
        tot = sb("tot", [P, 2, EXPERTS])
        wmean = sb("wmean", [P, 3, EXPERTS])
        wrow = sb("wrow", [P, MT])
        yT = sb("yT", [P, 2, GN])

        qf = sb("qf", [P, GN])
        kf = sb("kf", [P, GN])
        qres, kres = sg[:, 0, :], sg[0:KVH * DH, 1, :]
        qp = sb("qp", [P, 2, 3, GN], BF16)
        kp = sb("kp", [KVH * DH, 2, 3, GN], BF16)
        v_all = sb("v_all", [P, UNITS, SEQ // P, DH])
        qs = sb("qs", [P, 2, HPG, SEQ], BF16)
        ks = sb("ks", [P, 2, SEQ], BF16)
        vb = sb("vb", [P, 2, SEQ // P, 32])
        mx = sb("mx", [P, 2, 2, QT, HPG])
        mm_ = sb("mm_", [P, QT, HPG])
        wb = sb("wb", [P, QT, 2 * HPG], BF16)
        wt = sb("wt", [P, 2, HALF], BF16)
        osb = sb("osb", [P, 2, HALF])
        rden = sb("rden", [P, QT * HPG])
        attn = sb("attn", [P, UNITS, SEQ // P, HPG * DH])
        pr = h_all[:, 0:3, 0:HPG, :]
        masked = h_all[:, 3, 0:HPG // 2, :].rearrange("p a n -> p (a n)").bitcast(BF16)\
            .rearrange("p (a n) -> p a n", n=HALF)
        SW = TILES * EXPERTS
        choice = h_all[:, GROUPS - 1, 0:MT, :].rearrange("p a n -> p (a n)")
        lg, sc, *pick = [choice[:, n * SW:n * SW + SW].rearrange("p (t e) -> p t e", e=EXPERTS) for n in range(7)]
        top = [choice[:, 7 * SW + n * TILES:7 * SW + n * TILES + TILES] for n in range(7)]
        xnT_all = qs[:, :, :, :].rearrange("p a h n -> p (a h n)").bitcast(F32).rearrange("p (c n) -> p c n", n=GN)
        at_rows = attn[0:HEADS].rearrange("p u t e -> p (u t e)").bitcast(BF16)\
            .rearrange("p (r n) -> p r n", n=SEQ)
        h_rows = h_all[0:HEADS, GROUPS - 2, 0:MT, :].rearrange("p a n -> p (a n)").bitcast(BF16)\
            .rearrange("p (r n) -> p r n", n=SEQ)
        bias_st = [h_rows, at_rows[:, 0:4, :], at_rows[:, 4:8, :]]
        bias_f = h_all[0:HEADS, GROUPS - 1, 0:2, :].rearrange("p a n -> p (a n)")
        bias_r = h_all[0:HEADS, GROUPS - 1, 2:4, :].rearrange("p a n -> p (a n)")

        small_loads = [(c128, "c128"), (gate_w, "gate_w"), (lb, "lb"), (esel_f, "esel"), (slope[:, 0:1], "slopes"),
                       (qpos, "qpos")]
        ffn_loads = [(wg, "wg"), (wu, "wu")]
        late_loads = [(wd, "wd"), (krows, "krows"), (bq, "bq"), (bkv, "bkv"), (bo, "bo"), (wq, "wq"),
                      (wkv, "wkv"), (wo, "wo")]

        s_small = sem("s_small")
        s_w = sem("s_w")
        s_late = sem("s_late")
        s_x0 = sem("s_x0")
        s_init = sem("s_init")
        s_cb = sem("s_cb")
        s_bst = sem("s_bst")
        s_bdma0 = sem("s_bdma0")
        s_bdma = sem("s_bdma")
        s_dve = sem("s_dve")
        s_zero = sem("s_zero")
        s_kz = sem("s_kz")
        s_ks0 = sem("s_ks0")

        def ffn_sems(n):
            return FfnSems(*[sem(f"f{n}_{name}") for name in FFN_SEMS])

        f1, f2 = ffn_sems(1), ffn_sems(2)
        a_ld = [[sem("a_ld_first_even"), sem("a_ld_first_odd")], [sem("a_ld_second_even"), sem("a_ld_second_odd")]]
        a_vb = sem("a_vb")
        a_in = sem("a_in")
        a_out = sem("a_out")
        a_w = sem("a_w")
        a_wc = sem("a_wc")
        a_wp = sem("a_wp")
        a_wr = sem("a_wr")
        a_sc = sem("a_sc")
        a_ex = sem("a_ex")
        a_pv = sem("a_pv")
        a_ov = sem("a_ov")
        a_on = sem("a_on")
        a_ch = sem("a_ch")
        o_an, o_T, o_aT, o_y, o_x, o_bo = (sem(f"o_{n}") for n in ("an", "T", "aT", "y", "x", "bo"))

        block = ctx.enter_context(nc.Block())

        def xt(c):
            return x[:, bass.ds(c * GT, GT), :]

        def bank(b):
            return ps[:, b, :]

        @block.sync
        def _(sp):
            xd = dram["x"].rearrange("(c t p) f -> c p t f", t=GT, p=P)
            def load(names, s):
                for dst, name in names:
                    sp.dma_start(dst[tuple(slice(None) for _ in dst.shape)], dram[name]).then_inc(s, 16)

            sp.dma_start(x[:, 0:GT, :], xd[0]).then_inc(s_x0, 16)
            load(small_loads, s_small)
            load(ffn_loads, s_w)
            with sp.Fori(1, GROUPS) as c:
                sp.wait_ge(s_x0, 16 * c)
                sp.dma_start(xt(c), xd[c]).then_inc(s_x0, 16)
            load(late_loads, s_late)

            for part in range(3):
                sp.wait_ge(s_bst, part + 1)
                st = bias_st[part]
                s = s_bdma if part else s_bdma0
                for row in (0, 1):
                    sp.dma_start(bias_scr[:, 5 * part + row, :], st[:, 0, :]).then_inc(s, 16)
                sp.dma_start(bias_scr[:, 5 * part + 2:5 * part + 5, :], st[:, 1:4, :]).then_inc(s, 16)
            sp.dma_start(bias_scr[:, BIAS_ROWS, :], bias_st[2][:, 3, :]).then_inc(s_bdma, 16)
            sp.wait_ge(s_bdma0, 16 * 3)
            sp.wait_ge(s_bdma, 16 * 7)

            def store_parts(c, b, half):
                sp.wait_ge(f1.pq, c + 1)
                sp.wait_ge(f1.pk, c + 1)
                par = half
                n = slice(half * GN, half * GN + GN)
                dw = f1.dw1 if half else f1.dw0
                r = 0
                for part, products in RUNS:
                    sp.dma_start(q_scr[b, :, r:r + products, n],
                                 qp[:, par, part, None, :].broadcast_to([P, products, GN])).then_inc(dw, 16)
                    sp.dma_start(k_scr[b, :, r:r + products, n], kp[:, par, 0:products]).then_inc(dw, 16)
                    r += products

            def load_stack(i, par, g, half):
                s = a_ld[half][par]
                n = slice(half * HALF, half * HALF + HALF)
                sp.dma_start(qs[0:BIAS_ROWS + 1, par, :, n],
                             bias_scr[HPG * g:HPG * g + HPG, :, n].rearrange("h r n -> r h n")).then_inc(s, 16)
                sp.dma_start(ks[PROD:PROD + PRODS, par, n], k_units[i, :, n]).then_inc(s, 16)
                sp.dma_start(qs[PROD:PROD + PRODS, par, :, n],
                             q_units[i, :, :, n].rearrange("h m n -> m h n")).then_inc(s, 16)

            store_parts(0, 0, 0)
            store_parts(1, 0, 1)
            sp.wait_ge(f1.dw0, 16 * STORES)
            sp.wait_ge(f1.dw1, 16 * STORES)
            sp.wait_ge(s_kz, 2)
            sp.wait_ge(s_ks0, 1)
            for half in range(2):
                load_stack(0, 0, 0, half)
            for half in range(2):
                load_stack(1, 1, 1, half)
            with sp.Fori(1, BATCH) as b:
                store_parts(2 * b, b, 0)
                store_parts(2 * b + 1, b, 1)
            sp.wait_ge(f1.dw0, 16 * STORES * BATCH)
            sp.wait_ge(f1.dw1, 16 * STORES * BATCH)

            def reload(i, g):
                sp.wait_ge(a_pv, NSTEP * (i - 2) + 2 * QT)
                load_stack(i, g % 2, g, 0)
                sp.wait_ge(a_pv, NSTEP * (i - 1))
                load_stack(i, g % 2, g, 1)

            reload(2, 2)
            reload(3, 3)
            with sp.Fori(1, BATCH) as b:
                for g in range(KVH):
                    reload(KVH * b + g, g)
            od = out.rearrange("(c t p) f -> c p t f", t=GT, p=P)
            with sp.Fori(0, GROUPS) as c:
                sp.wait_ge(f2.x, c + 1)
                sp.dma_start(od[c], xt(c)).then_inc(f2.out, 16)
            sp.wait_ge(f2.out, 16 * GROUPS)

        @block.gpsimd
        def _(pool):
            pool.memset(mhalf[:, :], -0.5)
            pool.memset(ones[:, :], 1.0)
            pool.memset(mask_w[:, 0:HALF - P], 0.0)
            pool.memset(kf[:, :], 0.0)
            pool.memset(vb[:, :, :, :], 0.0).then_inc(s_init, 1)
            pool.wait_ge(s_init, 1)
            pool.memset(vb[:, :, :, DH:DH + 1], 1.0).then_inc(s_init, 1)

            def clear_keys():
                pool.wait_ge(s_init, 2)
                pool.memset(ks[:, :, :], 0.0).then_inc(s_kz, 1)
                pool.wait_ge(s_kz, 1)
                pool.memset(ks[WROW:P, :, :], 1.0).then_inc(s_kz, 1)
                pool.wait_ge(s_kz, 2)

            def rsqrt(c, par, ve_sem, xn_sem, rs_sem):
                pool.wait_ge(ve_sem, c + 1)
                after(pool, xn_sem, c - 1)
                pool.tensor_tensor(rstd[:, par, :], ve[:, par, :], mhalf[:, :], ALU.pow).then_inc(rs_sem, 1)
                pool.wait_ge(rs_sem, c + 1)

            def split(c, par):
                pool.wait_ge(f1.k0, c + 1)
                pool.tensor_tensor(kres, kf[0:KVH * DH, :], kp[:, par, 0, :], ALU.subtract)
                pool.tensor_tensor(kp[:, par, 1, :], kf[0:KVH * DH, :], kp[:, par, 0, :], ALU.subtract).then_inc(f1.ch_k, 1)
                pool.wait_ge(f1.ch_k, c + 1)
                pool.tensor_tensor(kp[:, par, 2, :], kres, kp[:, par, 1, :], ALU.subtract).then_inc(f1.pk, 1)
                pool.wait_ge(f1.pk, c + 1)

            def clear_queries(k):
                rows = qs[64:96, :, :, :].rearrange("p a h n -> p (a h) n")
                pool.memset(rows[:, 2 * k:2 * k + 2, :], 0.0).then_inc(s_zero, 1)
                pool.wait_ge(s_zero, k + 1)

            def down_body(c, par, first, last):
                rsqrt(c, par, f1.ve2, f1.xn2, f1.rs2)
                if not first:
                    split(c - 1, 1 - par)
                if isinstance(c, int):
                    clear_queries(3 if last else c)

            over_groups(pool, lambda c, par, first, last: rsqrt(c, par, f1.ve, f1.xn, f1.rs))
            clear_keys()
            pool.wait_ge(f1.U, HT * GROUPS)
            over_groups(pool, down_body)
            split(GROUPS - 1, 1)
            pool.wait_ge(s_late, 16 * len(late_loads))
            pool.wait_ge(f1.rs2, GROUPS)
            pool.wait_ge(f1.xn2, GROUPS)
            pool.tensor_tensor(x[:, :, :], x[:, :, :], bo[:, None, :].broadcast_to([P, TILES, P]), ALU.add)\
                .then_inc(o_bo, 1)
            pool.wait_ge(o_bo, 1)

            def write_rows(i, par, j):
                pool.wait_ge(a_wc, 2 * i + j + 1)
                for h in POOL_HEADS[j]:
                    ins = pool.tensor_tensor(qs[WROW:K2, par, h, HALF * j:HALF * j + HALF], wt[WROW:K2, j, :],
                                             onehot[WROW:K2, h:h + 1].broadcast_to([K2 - WROW, HALF]), ALU.mult)
                ins.then_inc(a_wp, 1)

            def rows_body(i, par, first, last):
                write_rows(i, par, 1)
                if not last:
                    write_rows(i + 1, 1 - par, 0)

            write_rows(0, 0, 0)
            over_units(pool, rows_body)
            pool.wait_ge(a_wp, 2 * UNITS)
            over_groups(pool, lambda c, par, first, last: rsqrt(c, par, f2.ve, f2.xn, f2.rs))

        @block.scalar
        def _(act):
            copy = ACT.Copy
            act.wait_ge(s_small, 16 * len(small_loads))
            act.activation(cb[:, :], c128[:, 0:3 * P], copy).then_inc(s_cb, 1)
            act.activation(mask_w[:, HALF - P:HALF], c128[:, P:2 * P], copy)
            act.activation(esel[:, :], esel_f[:, :], copy).then_inc(s_cb, 1)

            def stack_constants():
                act.wait_ge(s_late, 16 * len(late_loads))
                act.activation(bqs[:, :], bq[:, :], copy, scale=QSCALE).then_inc(s_cb, 1)
                act.wait_ge(s_kz, 1)
                act.activation(ks[0:BIAS_ROWS + 1, 0, :], krows[:, :], copy)
                act.activation(ks[0:BIAS_ROWS + 1, 1, :], krows[:, :], copy).then_inc(s_ks0, 1)
                act.wait_ge(s_cb, 3)

            def ffn_up(f):
                def silu(k, b):
                    act.wait_ge(f.G, k + 1)
                    after(act, f.h, k - 1)
                    act.activation(sg[:, b, :], bank(3 + b), ACT.Silu).then_inc(f.sg, 1)

                def front(c, par, first, last):
                    act.wait_ge(f.T, c + 1)
                    after(act, f.U, c - 1)
                    act.activation(xnT[:, par, :], bank(7 * par), copy).then_inc(f.xT, 1)
                    act.activation(xnT_all[:, c, :], bank(7 * par), copy).then_inc(f.xA, 1)
                    if not first:
                        silu(c - 1, 1 - par)

                def mask_T(c, par):
                    act.wait_ge(f.mT, c + 1)
                    after(act, f.G, 0 if isinstance(c, int) and c < 2 else GROUPS + MT * (c - 1))
                    act.activation(maskT[:, par, :], ps[0:EXPERTS, 2, 0:GN // 2].bitcast(BF16), copy)\
                       .then_inc(f.mk, 1)

                def routed_tiles(c, par, first, last):
                    for n in range(MT):
                        silu(GROUPS + MT * c + n, n % 2)
                        if n == 2 and not last:
                            mask_T(c + 1, 1 - par)

                over_groups(act, front)
                silu(GROUPS - 1, 1)
                act.wait_ge(f.lg, GROUPS)
                act.activation(sc, lg, ACT.Sigmoid).then_inc(f.sig, 1)
                mask_T(0, 0)
                over_groups(act, routed_tiles)

            def ffn_down(f, qkv):
                def y_T(c, par):
                    act.wait_ge(f.Y, c + 1)
                    after(act, f.T2, c - 1)
                    act.activation(yT[:, par, :], bank(par), copy).then_inc(f.yT, 1)

                def xn_T(c, par):
                    act.wait_ge(f.Tb, c + 1)
                    after(act, f.K, c - 1)
                    act.activation(xnT[:, par, :], bank(4), copy).then_inc(f.xTb, 1)

                def qk(c, par):
                    act.wait_ge(f.Q, c + 1)
                    after(act, f.pq, c)
                    after(act, f.dw1 if par else f.dw0, 8 * STORES * (c - par))
                    act.activation(qp[:, par, 0, :], bank(5), ACT.Identity, bias=bqs[:, 0:1], scale=QSCALE)
                    act.activation(qf[:, :], bank(5), ACT.Identity, bias=bqs[:, 0:1], scale=QSCALE)\
                       .then_inc(f.qf, 1)
                    act.wait_ge(f.K, c + 1)
                    after(act, f.pk, c)
                    after(act, f.V, c)
                    act.activation(kf[0:2 * KVH * DH, :], ps[0:2 * KVH * DH, 6, :], ACT.Identity, bias=bkv[:, 0:1])\
                       .then_inc(f.kf, 1)
                    act.activation(kp[:, par, 0, :], ps[0:KVH * DH, 6, :], ACT.Identity, bias=bkv[0:KVH * DH, 0:1])\
                       .then_inc(f.k0, 1)

                def body(c, par, first, last):
                    if qkv and not first:
                        xn_T(c - 1, 1 - par)
                    if not last:
                        y_T(c + 1, 1 - par)
                    if qkv and not first:
                        qk(c - 1, 1 - par)

                y_T(0, 0)
                over_groups(act, body)
                if qkv:
                    xn_T(GROUPS - 1, 1)
                    qk(GROUPS - 1, 1)

            def out_evac(i, j):
                act.wait_ge(a_pv, NSTEP * i + (QT if j == 0 else NSTEP))
                after(act, a_on, 2 * i + j - 1)
                act.activation(osb[:, j, :], bank(OBANK), copy).then_inc(a_ov, 1)

            def attention():
                def body(i, par, first, last):
                    for s, (j, kt) in enumerate(STEPS):
                        lo = max(0, kt - QT * j) * P
                        after(act, a_pv, NSTEP * i + s - 2)
                        for h in range(HPG):
                            m = HPG * s + h
                            act.wait_ge(a_sc, NEXP * i + m + 1)
                            act.activation(pr[:, s % 3, h, lo:HALF], ps[:, SBANK + m % 4, lo:HALF], ACT.Exp)\
                               .then_inc(a_ex, 1)
                        if s == 0 and not first:
                            out_evac(i - 1, 1)
                        if s == QT:
                            out_evac(i, 0)

                over_units(act, body)
                out_evac(UNITS - 1, 1)

            def out_proj():
                def body(c, par, first, last):
                    act.wait_ge(o_T, c + 1)
                    after(act, o_y, c - 1)
                    act.activation(yT[:, par, :], bank(par), copy).then_inc(o_aT, 1)
                over_groups(act, body)

            ffn_up(f1)
            stack_constants()
            ffn_down(f1, True)
            attention()
            out_proj()
            ffn_up(f2)
            ffn_down(f2, False)

        @block.vector
        def _(dve):
            V = ALU

            def slope_parts():
                ch = Chain(dve, s_dve)
                dve.wait_ge(s_small, 16 * len(small_loads))
                for part in range(3):
                    ch.link(dve.tensor_copy(sparts[:, part:part + 1], slope[:, part:part + 1]))
                    if part < 2:
                        ch.link(dve.tensor_tensor(slope[:, part + 1:part + 2], slope[:, part:part + 1],
                                                  sparts[:, part:part + 1], V.subtract))
                    ch.link(dve.tensor_scalar(slope[:, 4 + part:5 + part], sparts[:, part:part + 1], -1.0, None,
                                              V.mult))
                return ch

            def bias_rows(ch, part, step):
                st = bias_st[part]
                if step == 0:
                    ch.link(dve.tensor_scalar(bias_f, qpos[:, :], slope[:, 4 + part:5 + part], None, V.mult))
                    ch.link(dve.tensor_copy(st[:, 1, :], bias_f))
                elif step == 1:
                    ch.link(dve.tensor_tensor(bias_r, bias_f, st[:, 1, :], V.subtract))
                    ch.link(dve.tensor_copy(st[:, 2, :], bias_r))
                else:
                    dve.tensor_tensor(st[:, 3, :], bias_r, st[:, 2, :], V.subtract)
                    dve.tensor_scalar(st[:, 0, :], qpos[:, :], 0.0, slope[:, 4 + part:5 + part],
                                      V.mult, V.subtract).then_inc(s_bst, 1)

            def ln_stats(c, par, ch, s_ve):
                dve.memset(idle[:, 0:1], 0.0)
                for t in range(GT):
                    ins = dve.bn_stats(stats[:, par, t, :], x[:, c * GT + t, :])
                ch.link(ins)
                dve.memset(idle[:, 1:2], 0.0)
                for t in range(GT):
                    ins = dve.bn_aggr(mv[:, par, t, :], stats[:, par, t, :])
                ch.link(ins)
                dve.tensor_scalar(ve[:, par, :], mv[:, par, :, 1], EPS, None, V.add).then_inc(s_ve, 1)

            def ln_apply(c, par, s_rs, s_T, s_xn):
                after(dve, s_T, c)
                dve.wait_ge(s_rs, c + 1)
                for t in range(GT):
                    ins = dve.tensor_scalar(xn[:, t, :], x[:, c * GT + t, :], mv[:, par, t, 0:1],
                                            rstd[:, par, t:t + 1], V.subtract, V.mult)
                ins.then_inc(s_xn, 1)

            def ffn_up(f, load_sem):
                ch = Chain(dve, f.ch_up)
                LN_LINKS, TOP_LINKS = 2, 18

                def hidden(k, b, c, tile):
                    dve.wait_ge(f.U, k + 1)
                    dve.wait_ge(f.sg, k + 1)
                    dve.tensor_tensor(h_all[:, c, tile, :], bank(5 + b), sg[:, b, :], V.mult).then_inc(f.h, 1)

                def statistics(c, par):
                    ch.at(LN_LINKS * c)
                    if load_sem is not None:
                        dve.wait_ge(load_sem, 16 * c + 16)
                    ln_stats(c, par, ch, f.ve)

                def finish(c, par):
                    dve.wait_ge(f.gl, c + 1)
                    dve.tensor_tensor(lg[:, bass.ds(c * GT, GT), :],
                                      ps[:, 1 + par, 0:GT * EXPERTS].rearrange("p (t e) -> p t e", t=GT),
                                      lb[:, None, :].broadcast_to([P, GT, EXPERTS]), V.add).then_inc(f.lg, 1)
                    hidden(c, par, c, MT)

                def front(c, par, first, last):
                    if not last:
                        statistics(c + 1, 1 - par)
                    ln_apply(c, par, f.rs, f.T, f.xn)
                    if not isinstance(c, int) or c >= 2:
                        finish(c - 2, par)

                rk = rank[:, None, :].broadcast_to([P, TILES, EXPERTS])
                pick1, pick2, s2, eq, wt = pick
                m1, m2, r1, r2, den, w1, w2 = top

                def wide(a):
                    return a[:, :, None].broadcast_to([P, TILES, EXPERTS])

                def first_max(scores, m, r, sel):
                    ch.link(dve.tensor_reduce(m, scores, AX.X, V.max))
                    ch.link(dve.tensor_tensor(eq, scores, wide(m), V.is_equal))
                    ch.link(dve.tensor_tensor(eq, eq, rk, V.mult))
                    ch.link(dve.tensor_reduce(r, eq, AX.X, V.max))
                    ch.link(dve.tensor_tensor(sel, rk, wide(r), V.is_equal))

                def choose():
                    dve.wait_ge(f.sig, 1)
                    first_max(sc, m1, r1, pick1)
                    ch.link(dve.scalar_tensor_tensor(out=s2, in0=pick1, scalar=-4.0, in1=sc,
                                                     op0=V.mult, op1=V.add))
                    first_max(s2, m2, r2, pick2)
                    ch.link(dve.scalar_tensor_tensor(out=unsel[:, :, :], in0=pick1, scalar=-1.0, in1=pick2,
                                                     op0=V.add, op1=V.add))
                    mask(0, 0)

                def mask(c, par):
                    after(dve, f.mT, c - 1)
                    dve.tensor_copy(unsel_g[:, par, :, :], unsel[:, bass.ds(c * GT, GT), :]).then_inc(f.sel, 1)

                def weights():
                    dve.tensor_tensor(routed[:, :, 1, :], pick1, pick2, V.add)
                    ch.link(dve.tensor_tensor(den, m1, m2, V.add))
                    ch.link(dve.tensor_scalar(den, den, 1e-8, None, V.add))
                    ch.link(dve.reciprocal(den, den))
                    dve.tensor_tensor(w1, m1, den, V.mult)
                    ch.link(dve.tensor_tensor(w2, m2, den, V.mult))
                    dve.tensor_tensor(wt, pick1, wide(w1), V.mult)
                    ch.link(dve.tensor_tensor(s2, pick2, wide(w2), V.mult))
                    ch.link(dve.tensor_tensor(routed[:, :, 0, :], wt, s2, V.add))
                    assert ch.n == TOP_LINKS, ch.n
                    dve.tensor_reduce(tot[:, :, :], routed[:, :, :, :].rearrange("p t w e -> p w e t"), AX.X, V.add)\
                       .then_inc(f.tot, 1)

                def scale_down():
                    dve.wait_ge(f.tops, 1)
                    dve.wait_ge(s_late, 16 * len(late_loads))
                    t2 = ps[:, 1, 0:2 * EXPERTS].rearrange("p (w e) -> p w e", w=2)
                    ch.link(dve.tensor_scalar(wmean[:, 1, :], t2[:, 1, :], 1.0, None, V.max))
                    ch.link(dve.reciprocal(wmean[:, 2, :], wmean[:, 1, :]))
                    ch.link(dve.scalar_tensor_tensor(out=wmean[:, 0, :], in0=t2[:, 0, :], scalar=0.5,
                                                     in1=wmean[:, 2, :], op0=V.mult, op1=V.mult))
                    for k in range(2):
                        rows = slice(k * INTER, k * INTER + INTER)
                        ins = dve.tensor_copy(wrow[rows, :], wmean[rows, 0, k:EXPERTS:2])
                    ch.link(ins)
                    for i in range(MT):
                        dve.tensor_scalar(wds[:, i, :], wd[:, i, :], wrow[:, i:i + 1], None, V.mult)
                    dve.tensor_scalar(wds[:, MT, :], wd[:, MT, :], 0.5, None, V.mult).then_inc(f.wds, 1)

                def routed_tiles(c, par, first, last):
                    first_ffn = load_sem is not None
                    for n in range(MT):
                        hidden(GROUPS + MT * c + n, n % 2, c, n)
                        if n == 0 and not last:
                            mask(c + 1, 1 - par)
                        if n == 0 and first:
                            weights()
                        if n == 0 and isinstance(c, int) and c == 1:
                            scale_down()
                        if first_ffn and n and isinstance(c, int) and c < 3:
                            bias_rows(slopes, c, n - 1)
                    if first_ffn and isinstance(c, int) and c == 2:
                        dve.wait_ge(s_bdma0, 16 * 3)

                statistics(0, 0)
                over_groups(dve, front)
                finish(GROUPS - 2, 0)
                finish(GROUPS - 1, 1)
                ch.at(LN_LINKS * GROUPS)
                choose()
                over_groups(dve, routed_tiles)

            def ffn_down(f, qkv):
                ch = Chain(dve, f.ch_down)
                LN_LINKS, SPLIT_LINKS = 2, 2
                LINKS = LN_LINKS + SPLIT_LINKS

                def split(c, par):
                    dve.wait_ge(f.qf, c + 1)
                    ch.link(dve.tensor_tensor(qres, qf[:, :], qp[:, par, 0, :], V.subtract))
                    ch.link(dve.tensor_copy(qp[:, par, 1, :], qres))
                    dve.tensor_tensor(qp[:, par, 2, :], qres, qp[:, par, 1, :], V.subtract).then_inc(f.pq, 1)

                def values(c, b, half):
                    dve.wait_ge(f.V, c + 1)
                    vin = bank(7).rearrange("p (t w) -> p t w", t=GT)[:, :, KVH * DH:2 * KVH * DH]\
                        .rearrange("p t (g d) -> p g t d", g=KVH)
                    dve.tensor_copy(v_all[:, bass.ds(KVH * b, KVH), GT * half:GT * half + GT, :], vin)\
                       .then_inc(f.v, 1)

                def body(c, par, first, last, batch=None):
                    if batch is not None:
                        values(c - 2, batch, par)
                    dve.wait_ge(f.T2, c + 1)
                    dve.tensor_tensor(xt(c), xt(c), bank(2 + par).rearrange("p (t f) -> p t f", t=GT), V.add)\
                       .then_inc(f.x, 1)
                    if qkv:
                        ch.at(0 if first else LINKS * c - SPLIT_LINKS)
                        dve.wait_ge(f.x, c + 1)
                        ln_stats(c, par, ch, f.ve2)
                        ln_apply(c, par, f.rs2, f.Tb, f.xn2)
                        if last:
                            for n in EARLY[0]:
                                reduce(n)
                        if not first:
                            split(c - 1, 1 - par)

                if not qkv:
                    over_groups(dve, body)
                    return
                body(0, 0, True, False)
                body(1, 1, False, False)
                body(2, 0, False, False, 0)
                with dve.Fori(1, (GROUPS - 2) // 2) as r:
                    body(2 * r + 1, 1, False, False, r - 1)
                    body(2 * r + 2, 0, False, False, r)
                body(GROUPS - 1, 1, False, True, BATCH - 2)
                values(GROUPS - 2, BATCH - 1, 0)
                for n in EARLY[1]:
                    reduce(n)
                ch.at(LINKS * GROUPS - SPLIT_LINKS)
                split(GROUPS - 1, 1)
                values(GROUPS - 1, BATCH - 1, 1)

            ring = Ring()

            def reduce(n):
                t, h, per, k0, w, diag = PIECES[n]
                b, done = ring.take()
                dve.wait_ge(a_in, done + 1)
                m = mx[:, t // QT, 0 if diag else 1, t % QT, h:h + per]
                if diag and per == 1:
                    dve.wait_ge(a_out, done - 3)
                    dve.memset(idle[:, 4 + h:5 + h], 0.0)
                    dve.tensor_tensor_reduce(out=masked[:, h, 0:w], in0=ps[:, b, 0:w],
                                             in1=mask_w[:, HALF - w:HALF], scale=1.0, scalar=LOWEST,
                                             op0=V.add, op1=V.max, accum_out=m).then_inc(a_out, 1)
                else:
                    src = ps[:, b, 0:per * w].rearrange("p (h w) -> p h w", h=per)
                    dve.tensor_reduce(m, src, AX.X, V.max).then_inc(a_out, 1)
                return done + 1

            def attention():
                ch = Chain(dve, a_ch)

                def load_v(i, par):
                    after(dve, a_pv, NSTEP * (i - 1))
                    dve.tensor_copy(vb[:, par, :, 0:DH], v_all[:, i, :, :]).then_inc(a_vb, 1)

                def rows_out(i, par, j):
                    b, done = ring.take()
                    dve.wait_ge(a_in, done + 1)
                    after(dve, a_wp, 2 * i + j - 1)
                    dve.tensor_copy(wt[WROW:K2, j, :], ps[WROW:K2, b, 0:HALF // 2].bitcast(BF16)).then_inc(a_wc, 1)
                    dve.wait_ge(a_wc, 2 * i + j + 1)
                    dve.memset(idle[:, 0:1], 0.0).then_inc(a_out, 1)
                    if j:
                        for h in range(POOL_HEADS[1][0]):
                            ins = dve.tensor_scalar(qs[WROW:K2, par, h, HALF:SEQ], wt[WROW:K2, 1, :],
                                                    onehot[WROW:K2, h:h + 1], None, V.mult)
                        ins.then_inc(a_wr, 1)

                def maxima(i, j, done):
                    dve.wait_ge(a_out, done)
                    m = mx[:, 0, 0]
                    if j:
                        m = mm_[:, :, :]
                        ch.link(dve.tensor_tensor(m, mx[:, 1, 0], mx[:, 1, 1], V.max))
                    after(dve, a_wc, 2 * i + j)
                    ch.link(dve.tensor_scalar(wb[:, :, 0:HPG], m, -1.0, None, V.mult))
                    dve.scalar_tensor_tensor(out=wb[:, :, HPG:2 * HPG], in0=m, scalar=-1.0, in1=wb[:, :, 0:HPG],
                                             op0=V.mult, op1=V.subtract).then_inc(a_w, 1)

                def normalise(i, j):
                    b, done = ring.take()
                    after(dve, a_on, 2 * i + j)
                    dve.wait_ge(a_in, done + 1)
                    o = bank(b).rearrange("p (m e) -> p m e", m=QT * HPG)
                    ch.link(dve.reciprocal(rden[:, :], o[:, :, DH]))
                    dve.tensor_tensor(
                        attn[:, i, QT * j:QT * j + QT, :].rearrange("p t (h d) -> p (t h) d", h=HPG),
                        o[:, :, 0:DH], rden[:, :, None].broadcast_to([P, QT * HPG, DH]), V.mult)\
                       .then_inc(a_on, 1)
                    dve.wait_ge(a_on, 2 * i + j + 1)
                    dve.memset(idle[:, 0:1], 0.0).then_inc(a_out, 1)

                load_v(0, 0)
                for n in range(EARLY[1][-1] + 1, NP1):
                    done = reduce(n)
                    if n == FIRST_HALF - 1:
                        maxima(0, 0, done)
                    if n == START_T:
                        rows_out(0, 0, 0)
                maxima(0, 1, done)
                START_LINKS = 3
                UNIT_LINKS = 2 + 3

                def body(i, par, first, last):
                    ch.at(START_LINKS + UNIT_LINKS * i - (0 if first else 1))
                    ring.unit(i, first)
                    if not last:
                        load_v(i + 1, 1 - par)
                    for s in range(NSTEP):
                        if not last:
                            for n in range(STEP_START[s], STEP_START[s] + PER_STEP[s]):
                                done = reduce(n)
                                if n == FIRST_HALF - 1:
                                    maxima(i + 1, 0, done)
                        if s == W1_STEP:
                            rows_out(i, par, 1)
                        if s == OT1_STEP and not first:
                            normalise(i - 1, 1)
                        if s == OT0_STEP:
                            normalise(i, 0)
                        if s == W0_STEP and not last:
                            rows_out(i + 1, 1 - par, 0)
                    if not last:
                        maxima(i + 1, 1, done)

                over_units(dve, body)
                normalise(UNITS - 1, 1)

            def out_proj():
                def gather(c, b, half, par):
                    after(dve, o_T, c - 1)
                    src = attn[:, bass.ds(KVH * b, KVH), GT * half:GT * half + GT, :]
                    dve.tensor_copy(sg[:, par, :].rearrange("p (t g e) -> p g t e", t=GT, g=KVH), src)\
                       .then_inc(o_an, 1)

                def residual(c, par):
                    dve.wait_ge(o_y, c + 1)
                    dve.tensor_tensor(xt(c), xt(c), bank(2 + par).rearrange("p (t f) -> p t f", t=GT), V.add)\
                       .then_inc(o_x, 1)

                dve.wait_ge(a_on, 2 * UNITS)
                dve.wait_ge(o_bo, 1)
                gather(0, 0, 0, 0)
                gather(1, 0, 1, 1)
                gather(2, 1, 0, 0)
                residual(0, 0)
                gather(3, 1, 1, 1)
                residual(1, 1)
                with dve.Fori(1, BATCH - 1) as b:
                    gather(2 * b + 2, b + 1, 0, 0)
                    residual(2 * b, 0)
                    gather(2 * b + 3, b + 1, 1, 1)
                    residual(2 * b + 1, 1)
                residual(GROUPS - 2, 0)
                residual(GROUPS - 1, 1)
                dve.wait_ge(o_x, GROUPS)

            slopes = slope_parts()
            ffn_up(f1, s_x0)
            ffn_down(f1, True)
            attention()
            out_proj()
            ffn_up(f2, None)
            ffn_down(f2, False)

        @block.tensor
        def _(pe):
            def mm(o, l, r, start=True, stop=True):
                return pe.matmul(o, l, r, start=start, stop=stop, skip_group_check=True)

            def turn(src, b):
                for t in range(GT):
                    ins = pe.transpose(ps[:, b, t * P:(t + 1) * P], src(t), ident)
                return ins

            def ffn_up(f):
                def gate_and_up(k, b, tile, xT):
                    after(pe, f.sg, k - 1)
                    mm(bank(3 + b), wg[:, tile, :], xT, stop=False)
                    after(pe, f.h, k - 1)
                    mm(bank(5 + b), wu[:, tile, :], xT).then_inc(f.U, 1)

                def mask_gate(b, tile, mask):
                    mm(bank(3 + b), esel[:, tile * P:(tile + 1) * P], mask, start=False).then_inc(f.G, 1)

                def up(k, b, tile, xT, mask):
                    after(pe, f.sg, k - 1)
                    ins = mm(bank(3 + b), wg[:, tile, :], xT, stop=mask is None)
                    if mask is not None:
                        ins = mm(bank(3 + b), esel[:, tile * P:(tile + 1) * P], mask, start=False)
                    ins.then_inc(f.G, 1)
                    after(pe, f.h, k - 1)
                    mm(bank(5 + b), wu[:, tile, :], xT).then_inc(f.U, 1)

                def front(c, par, first, last):
                    pe.wait_ge(f.xn, c + 1)
                    after(pe, f.xA, c - 1)
                    turn(lambda t: xn[:, t, :], 7 * par).then_inc(f.T, 1)
                    if first:
                        pe.wait_ge(s_w, 16 * len(ffn_loads))
                    else:
                        up(c - 1, 1 - par, MT, xnT[:, 1 - par, :], None)
                    pe.wait_ge(f.xT, c + 1)
                    after(pe, f.lg, c - 1)
                    for t in range(GT):
                        ins = mm(ps[:, 1 + par, EXPERTS * t:EXPERTS * t + EXPERTS], xnT[:, par, t * P:(t + 1) * P],
                                 gate_w[:, :])
                    ins.then_inc(f.gl, 1)

                def mask_T(c, par):
                    pe.wait_ge(f.sel, c + 1)
                    after(pe, f.mk, c)
                    o = ps[0:EXPERTS, 2, 0:GN // 2].bitcast(BF16)
                    for t in range(GT):
                        ins = pe.transpose(o[:, t * P:(t + 1) * P], unsel_g[:, par, t, :], ident_b)
                    ins.then_inc(f.mT, 1)

                def routed_tiles(c, par, first, last):
                    late = 2 if first else 1
                    for n in range(late):
                        gate_and_up(GROUPS + MT * c + n, n % 2, n, xnT_all[:, c, :])
                    if first:
                        mask_T(0, 0)
                    pe.wait_ge(f.mk, c + 1)
                    for n in range(late):
                        mask_gate(n % 2, n, maskT[:, par, :])
                    for n in range(late, MT):
                        up(GROUPS + MT * c + n, n % 2, n, xnT_all[:, c, :], maskT[:, par, :])
                        if n == late and not last:
                            mask_T(c + 1, 1 - par)
                    if first:
                        pe.wait_ge(f.tot, 1)
                        mm(ps[:, 1, 0:2 * EXPERTS], ones[:, :], tot[:, :, :].rearrange("p w e -> p (w e)"))\
                            .then_inc(f.tops, 1)

                over_groups(pe, front)
                up(GROUPS - 1, 1, MT, xnT[:, 1, :], None)
                pe.wait_ge(f.xA, GROUPS)
                over_groups(pe, routed_tiles)

            def ffn_down(f, qkv):
                def down(c, par, transpose=0):
                    after(pe, f.yT, c - 1)
                    for i in range(HT):
                        if transpose > 1 and i == 2:
                            v_T(c - 3)
                        if transpose and i == HT // 2 + 1:
                            xn_T(c - 2)
                        ins = mm(bank(par), wds[:, i, :], h_all[:, c, i, :], start=(i == 0), stop=(i == HT - 1))
                    ins.then_inc(f.Y, 1)

                def project(c, par):
                    pe.wait_ge(f.xTb, c + 1)
                    after(pe, f.qf, c)
                    mm(bank(5), wq[:, :], xnT[:, par, :]).then_inc(f.Q, 1)
                    after(pe, f.k0, c)
                    mm(ps[0:2 * KVH * DH, 6, :], wkv[:, :], xnT[:, par, :]).then_inc(f.K, 1)

                def v_T(c):
                    pe.wait_ge(f.kf, c + 1)
                    after(pe, f.v, c)
                    turn(lambda t: kf[:, t * P:(t + 1) * P], 7).then_inc(f.V, 1)

                def xn_T(c):
                    pe.wait_ge(f.xn2, c + 1)
                    after(pe, f.xTb, c)
                    turn(lambda t: xn[:, t, :], 4).then_inc(f.Tb, 1)

                def body(c, par, first, last):
                    if not last:
                        down(c + 1, 1 - par, 0 if first or not qkv else 1 if isinstance(c, int) and c == 1 else 2)
                    pe.wait_ge(f.yT, c + 1)
                    after(pe, f.x, c - 1)
                    turn(lambda t: yT[:, par, t * P:(t + 1) * P], 2 + par).then_inc(f.T2, 1)
                    if qkv and last:
                        v_T(c - 2)
                        xn_T(c - 1)
                        pe.wait_ge(a_ld[0][0], 16 * LOADS)
                        pe.wait_ge(s_zero, 2)
                        pe.wait_ge(s_ks0, 1)
                        pe.wait_ge(f.x, GROUPS)
                        for n in EARLY[0]:
                            piece(n, 0)
                    if qkv and not first:
                        project(c - 1, 1 - par)

                pe.wait_ge(f.wds, 1)
                down(0, 0)
                over_groups(pe, body)
                if qkv:
                    xn_T(GROUPS - 1)
                    v_T(GROUPS - 2)
                    for n in EARLY[1]:
                        piece(n, 0)
                    project(GROUPS - 1, 1)
                    for n in EARLY[2]:
                        piece(n, 0)
                    v_T(GROUPS - 1)

            ring = Ring()

            def slot():
                b, done = ring.take()
                after(pe, a_out, done - RING + 1)
                return b

            def piece(n, par):
                t, h0, per, k0, w, diag = PIECES[n]
                diag = diag and per > 1
                b = slot()
                for k in range(per):
                    ins = mm(ps[:, b, k * w:k * w + w], qs[0:K1, par, h0 + k, t * P:(t + 1) * P],
                             ks[0:K1, par, k0:k0 + w], stop=not diag)
                    if diag:
                        ins = mm(ps[:, b, k * w + w - P:k * w + w], ident_b, mask_qk, start=False)
                ins.then_inc(a_in, 1)

            def maxima_T(i, j):
                b = slot()
                pe.wait_ge(a_w, 2 * i + j + 1)
                o = ps[WROW:K2, b, 0:HALF // 2].bitcast(BF16)
                for t in range(QT):
                    ins = pe.transpose(o[:, t * P:(t + 1) * P], wb[:, t, :], ident_b)
                ins.then_inc(a_in, 1)

            def out_T(i, j):
                b = slot()
                pe.wait_ge(a_ov, 2 * i + j + 1)
                turn(lambda t: osb[:, j, t * P:(t + 1) * P], b).then_inc(a_in, 1)

            def score(i, s, h, par):
                j, kt = STEPS[s]
                m = HPG * s + h
                lo = max(0, kt - QT * j) * P
                diag = kt >= QT * j
                after(pe, a_ex, NEXP * i + m - 3)
                b = SBANK + m % 4
                ins = mm(ps[:, b, lo:HALF], ks[0:K2, par, kt * P:(kt + 1) * P],
                         qs[0:K2, par, h, HALF * j + lo:HALF * j + HALF], stop=not diag)
                if diag:
                    ins = mm(ps[:, b, lo:lo + P], ident_b, mask_kq, start=False)
                ins.then_inc(a_sc, 1)

            def times_v(i, s, par):
                j, kt = STEPS[s]
                lo = max(0, kt - QT * j) * P
                last = kt == QT * (j + 1) - 1
                pe.wait_ge(a_ex, NEXP * i + HPG * (s + 1))
                if kt == 0:
                    after(pe, a_ov, 2 * i + j)
                for h in range(HPG):
                    ins = mm(ps[32 * h:32 * h + 32, OBANK, lo:HALF], vb[:, par, kt, :], pr[:, s % 3, h, lo:HALF],
                             start=(kt == 0), stop=last)
                ins.then_inc(a_pv, 1)

            def attention():
                def next_stack(i, par, half):
                    pe.wait_ge(a_ld[half][1 - par], 8 * LOADS * (i + 3 if par else i + 2))

                pe.wait_ge(a_ld[1][0], 16 * LOADS)
                for n in range(EARLY[2][-1] + 1, NP1):
                    piece(n, 0)
                    if n == START_T:
                        maxima_T(0, 0)
                pe.wait_ge(a_wp, 1)
                pe.wait_ge(s_zero, 4)
                pe.wait_ge(f1.k0, GROUPS)
                pe.wait_ge(f1.v, GROUPS)
                for h in range(HPG):
                    score(0, 0, h, 0)

                def body(i, par, first, last):
                    ring.unit(i, first)
                    pe.wait_ge(a_vb, i + 1)
                    for s in range(NSTEP):
                        todo = [] if last else list(range(STEP_START[s], STEP_START[s] + PER_STEP[s]))
                        if s + 1 == QT:
                            pe.wait_ge(a_wp, 2 * i + 2)
                            pe.wait_ge(a_wr, i + 1)
                        if s + 1 == NSTEP and not last:
                            pe.wait_ge(a_wp, 2 * i + 3)
                        if 0 in todo:
                            next_stack(i, par, 0)
                        for h in range(HPG):
                            if h < len(todo) and todo[h] == FIRST_HALF:
                                next_stack(i, par, 1)
                            if s + 1 < NSTEP:
                                score(i, s + 1, h, par)
                            elif not last:
                                score(i + 1, 0, h, 1 - par)
                            if h < len(todo):
                                piece(todo[h], 1 - par)
                        times_v(i, s, par)
                        if s == W1_STEP:
                            maxima_T(i, 1)
                        if s == OT1_STEP and not first:
                            out_T(i - 1, 1)
                        if s == OT0_STEP:
                            out_T(i, 0)
                        if s == W0_STEP and not last:
                            maxima_T(i + 1, 0)

                over_units(pe, body)
                out_T(UNITS - 1, 1)

            def out_proj():
                def attention_T(c, par):
                    pe.wait_ge(o_an, c + 1)
                    after(pe, o_aT, c - 1)
                    turn(lambda t: sg[:, par, t * P:(t + 1) * P], par).then_inc(o_T, 1)

                def body(c, par, first, last):
                    if not last:
                        attention_T(c + 1, 1 - par)
                    pe.wait_ge(o_aT, c + 1)
                    after(pe, o_x, c - 1)
                    for t in range(GT):
                        ins = mm(ps[:, 2 + par, t * P:(t + 1) * P], yT[:, par, t * P:(t + 1) * P], wo[:, :])
                    ins.then_inc(o_y, 1)

                attention_T(0, 0)
                over_groups(pe, body)

            pe.wait_ge(s_small, 16 * len(small_loads))
            pe.wait_ge(s_cb, 2)
            pe.wait_ge(s_init, 2)
            ffn_up(f1)
            pe.wait_ge(s_late, 16 * len(late_loads))
            ffn_down(f1, True)
            attention()
            out_proj()
            ffn_up(f2)
            ffn_down(f2, False)


def kernel(L0_attn_qkv, L0_attn_Wq, L0_attn_bq, L0_attn_Wk, L0_attn_bk, L0_attn_Wv, L0_attn_bv, L0_attn_Wo,
           L0_attn_bo, L0_attn_slopes, L0_ffn_gate_w, L0_ffn_lb_bias, L0_ffn_expert_gate_w, L0_ffn_expert_up_w,
           L0_ffn_expert_down_w, L0_ffn_shared_gate_w, L0_ffn_shared_up_w, L0_ffn_shared_down_w):
    import numpy as np
    import concourse.bacc as bacc
    from concourse.bass_utils import run_bass_kernel_spmd

    def arr(a):
        return np.ascontiguousarray(np.asarray(a))

    at = np.arange(P)
    c128 = np.zeros((P, 3 * P + HPG + EXPERTS), np.float32)
    c128[:, 0:P] = np.eye(P)
    c128[:, P:2 * P] = np.where(at[None, :] > at[:, None], -1e30, 0.0)
    c128[:, 2 * P:3 * P] = np.where(at[:, None] > at[None, :], -1e30, 0.0)
    for h in range(HPG):
        c128[[WROW + h, WROW + HPG + h], 3 * P + h] = 1.0
    c128[:, 3 * P + HPG:] = np.arange(EXPERTS, 0, -1)
    pos = np.arange(SEQ, dtype=np.float32)
    krows = np.zeros((BIAS_ROWS + 1, SEQ), np.float32)
    for part in range(3):
        krows[5 * part] = pos - pos % 8
        krows[5 * part + 1] = pos % 8
        krows[5 * part + 2:5 * part + 5] = 1.0
    esel = np.zeros((EXPERTS, MT, P), np.float32)
    for e in range(EXPERTS):
        esel[e, e // 2, (e % 2) * INTER:(e % 2) * INTER + INTER] = 2.0 ** 30

    def up(experts, shared):
        w = np.concatenate([arr(experts).reshape(EXPERTS * INTER, DM), arr(shared)], 0)
        return arr(w.T.reshape(DM, HT, P))

    down = np.concatenate([arr(L0_ffn_expert_down_w).transpose(0, 2, 1).reshape(EXPERTS * INTER, DM),
                           arr(L0_ffn_shared_down_w).T], 0)
    data = {
        "x": arr(L0_attn_qkv).reshape(BATCH * SEQ, DM),
        "slopes": arr(L0_attn_slopes).reshape(HEADS, 1),
        "c128": c128, "krows": krows, "qpos": arr(np.broadcast_to(pos, (HEADS, SEQ))),
        "esel": esel.reshape(EXPERTS, MT * P),
        "gate_w": arr(arr(L0_ffn_gate_w).T),
        "lb": arr(np.broadcast_to(arr(L0_ffn_lb_bias), (P, EXPERTS))),
        "bq": arr(L0_attn_bq).reshape(DM, 1), 
        "bkv": arr(np.concatenate([arr(L0_attn_bk), arr(L0_attn_bv)])).reshape(2 * KVH * DH, 1),
        "bo": arr(np.broadcast_to(arr(L0_attn_bo), (P, DM))),
        "wg": up(L0_ffn_expert_gate_w, L0_ffn_shared_gate_w),
        "wu": up(L0_ffn_expert_up_w, L0_ffn_shared_up_w),
        "wd": arr(down.reshape(HT, P, DM).transpose(1, 0, 2)),
        "wq": arr(L0_attn_Wq), "wkv": arr(np.concatenate([arr(L0_attn_Wk), arr(L0_attn_Wv)], 1)),
        "wo": arr(L0_attn_Wo),
    }
    nc = bacc.Bacc("TRN2", target_bir_lowering=False, num_devices=1)
    dram = {n: nc.dram_tensor(f"in_{n}", a.shape, F32, kind="ExternalInput").ap() for n, a in data.items()}
    out = nc.dram_tensor("out", (BATCH * SEQ, DM), F32, kind="ExternalOutput").ap()
    macaron(nc, dram, out)
    r = run_bass_kernel_spmd(nc, [{f"in_{n}": a for n, a in data.items()}], core_ids=[0])
    return r.results[0]["out"].reshape(BATCH, SEQ, DM)
```
